# Optimizing a Trainium2 kernel written in Bass

```python
import numpy as np
import jax
import jax.numpy as jnp

def _softmax(x, axis=-1):
    return jax.nn.softmax(x, axis=axis)

def _gelu(x):
    return jax.nn.gelu(x, approximate=True)

def _silu(x):
    return jax.nn.silu(x)

def _sigmoid(x):
    return jax.nn.sigmoid(x)

def _layernorm(x, axis=-1, eps=1e-05):
    m = jnp.mean(x, axis=axis, keepdims=True)
    v = jnp.var(x, axis=axis, keepdims=True)
    return (x - m) / jnp.sqrt(v + eps)

def _scatter_add(tgt, idx, src, axis=0):
    return tgt.at[idx].add(src)

def _segment_sum(src, seg, n):
    return jax.ops.segment_sum(src, seg, n)
kernel_name = 'mk_gnn_resnorm_d4_gnn_r32_dcb172'

def setup_inputs(seed: int=0):
    np.random.seed(seed)
    _w = jnp.asarray

    def _rec_inputs():
        import jax
        import jax.numpy as jnp
        _gk = jax.random.key(seed)
        x = -0.0003713 + 1 * jax.random.normal(jax.random.fold_in(_gk, 1), (3125, 256), jnp.float32)
        src = jax.random.randint(jax.random.fold_in(_gk, 2), (50000,), 0, 3125, jnp.int32)
        dst = jax.random.randint(jax.random.fold_in(_gk, 3), (50000,), 0, 3125, jnp.int32)
        _o = jnp.argsort(dst, stable=True)
        src = src[_o]
        dst = dst[_o]
        return (x, src, dst)
    x, src, dst = _rec_inputs()

    def _L0_gnn_setup():
        import jax, jax.numpy as jnp
        import numpy as np
        N_NODES = 50000
        N_EDGES = 25000
        D_IN = 256
        D_HID = 256
        D_OUT = 256
        GAMMA = 0.0
        K_STEPS = 6

        def _spmm(h, src, dst, inv_deg):
            msg = h[src]
            agg = jax.ops.segment_sum(msg, dst, num_segments=h.shape[0])
            return agg * inv_deg[:, None]

        def _linear_diffusion(h, src, dst, gamma=GAMMA, k=K_STEPS):
            n = h.shape[0]
            deg = jax.ops.segment_sum(jnp.ones((src.shape[0],), h.dtype), dst, num_segments=n)
            inv_deg = 1.0 / jnp.clip(deg, 1.0)
            out = h
            term = h
            for i in range(1, k + 1):
                term = (_spmm(term, src, dst, inv_deg) + gamma * term) / float(i)
                out = out + term
            return out
        key = jax.random.key(seed)
        ks = jax.random.split(key, 8)
        h = jax.random.normal(ks[0], (N_NODES, D_IN), dtype=jnp.float32)
        src = jax.random.randint(ks[1], (N_EDGES,), 0, N_NODES, dtype=jnp.int64)
        dst = jax.random.randint(ks[2], (N_EDGES,), 0, N_NODES, dtype=jnp.int64)
        s_in = 1.0 / np.sqrt(D_IN)
        s_hid = 1.0 / np.sqrt(D_HID)
        W_in = jax.random.uniform(ks[3], (D_HID, D_IN), jnp.float32, -s_in, s_in)
        b_in = jax.random.uniform(ks[4], (D_HID,), jnp.float32, -s_in, s_in)
        W_out = jax.random.uniform(ks[5], (D_OUT, D_HID), jnp.float32, -s_hid, s_hid)
        b_out = jax.random.uniform(ks[6], (D_OUT,), jnp.float32, -s_hid, s_hid)
        return {'h': h, 'src': src, 'dst': dst, 'W_in': W_in, 'b_in': b_in, 'W_out': W_out, 'b_out': b_out}
    _L0_gnn_all = _L0_gnn_setup()
    _L0_gnn_in = {k: v for k, v in _L0_gnn_all.items() if k in ('W_in', 'b_in', 'W_out', 'b_out')}
    del _L0_gnn_all

    def _L1_gnn_setup():
        import jax, jax.numpy as jnp
        import numpy as np
        N = 50000
        E = 25000
        D_IN = 256
        HID = 32
        HEADS = 8
        D_OUT = 64
        NEG_SLOPE = 0.2

        def _gat_conv(x, src, dst, W, att_src, att_dst, bias, heads, out_dim, concat):
            n = x.shape[0]
            h = (x @ W.T).reshape(n, heads, out_dim)
            a_s = jnp.sum(h * att_src, axis=-1)
            a_d = jnp.sum(h * att_dst, axis=-1)
            logits = jax.nn.leaky_relu(a_s[src] + a_d[dst], NEG_SLOPE)
            m = jax.ops.segment_max(logits, dst, num_segments=n)
            e = jnp.exp(logits - m[dst])
            den = jax.ops.segment_sum(e, dst, num_segments=n)
            alpha = e / (den[dst] + 1e-16)
            out = jax.ops.segment_sum(alpha[:, :, None] * h[src], dst, num_segments=n)
            out = out.reshape(n, heads * out_dim) if concat else out.mean(axis=1)
            return out + bias
        key = jax.random.key(seed)
        ks = jax.random.split(key, 12)
        x = jax.random.normal(ks[0], (N, D_IN), jnp.float32)
        edge_index = jax.random.randint(ks[1], (2, E), 0, N, dtype=jnp.int32)
        g = lambda k, shape, fan_in: jax.random.normal(k, shape, jnp.float32) / np.sqrt(fan_in)
        W0 = g(ks[2], (HEADS * HID, D_IN), D_IN)
        att_src0 = g(ks[3], (1, HEADS, HID), HID)
        att_dst0 = g(ks[4], (1, HEADS, HID), HID)
        b0 = jnp.zeros((HEADS * HID,), jnp.float32)
        W1 = g(ks[5], (1 * D_OUT, HEADS * HID), HEADS * HID)
        att_src1 = g(ks[6], (1, 1, D_OUT), D_OUT)
        att_dst1 = g(ks[7], (1, 1, D_OUT), D_OUT)
        b1 = jnp.zeros((D_OUT,), jnp.float32)
        return {'x': x, 'edge_index': edge_index, 'W0': W0, 'att_src0': att_src0, 'att_dst0': att_dst0, 'b0': b0, 'W1': W1, 'att_src1': att_src1, 'att_dst1': att_dst1, 'b1': b1}
    _L1_gnn_all = _L1_gnn_setup()
    _L1_gnn_in = {k: v for k, v in _L1_gnn_all.items() if k in ('W0', 'att_src0', 'att_dst0', 'b0', 'W1', 'att_src1', 'att_dst1', 'b1')}
    del _L1_gnn_all

    def _L2_gnn_setup():
        import jax, jax.numpy as jnp
        import numpy as np
        N = 50000
        E = 25000
        HEADS = 4
        C = 64
        IN = 256
        NEG_SLOPE = 0.2

        def _gat_forward(x, edge_index, W, att_src, att_dst, bias):
            n = x.shape[0]
            h = (x @ W).reshape(n, HEADS, C)
            loop = jnp.arange(n, dtype=edge_index.dtype)
            src = jnp.concatenate([edge_index[0], loop])
            dst = jnp.concatenate([edge_index[1], loop])
            a_src = jnp.einsum('nhc,hc->nh', h, att_src)
            a_dst = jnp.einsum('nhc,hc->nh', h, att_dst)
            logits = a_src[src] + a_dst[dst]
            logits = jnp.where(logits >= 0, logits, NEG_SLOPE * logits)
            seg_max = jax.ops.segment_max(logits, dst, num_segments=n)
            seg_max = jnp.where(jnp.isfinite(seg_max), seg_max, 0.0)
            ex = jnp.exp(logits - seg_max[dst])
            denom = jax.ops.segment_sum(ex, dst, num_segments=n)
            alpha = ex / (denom[dst] + 1e-16)
            msgs = alpha[:, :, None] * h[src]
            out = jax.ops.segment_sum(msgs, dst, num_segments=n)
            out = out.reshape(n, HEADS * C) + bias
            return jax.nn.relu(out)
        key = jax.random.key(seed)
        k = jax.random.split(key, 6)
        x = jax.random.normal(k[0], (N, IN), dtype=jnp.float32)
        edge_index = jax.random.randint(k[1], (2, E), 0, N, dtype=jnp.int64)
        W = jax.random.normal(k[2], (IN, HEADS * C), dtype=jnp.float32) * (1.0 / np.sqrt(IN))
        att_src = jax.random.normal(k[3], (HEADS, C), dtype=jnp.float32) * (1.0 / np.sqrt(C))
        att_dst = jax.random.normal(k[4], (HEADS, C), dtype=jnp.float32) * (1.0 / np.sqrt(C))
        bias = jax.random.normal(k[5], (HEADS * C,), dtype=jnp.float32) * 0.02
        return {'x': x, 'edge_index': edge_index, 'W': W, 'att_src': att_src, 'att_dst': att_dst, 'bias': bias}
    _L2_gnn_all = _L2_gnn_setup()
    _L2_gnn_in = {k: v for k, v in _L2_gnn_all.items() if k in ('W', 'att_src', 'att_dst', 'bias')}
    del _L2_gnn_all

    def _L3_gnn_setup():
        import jax, jax.numpy as jnp
        import numpy as np
        N, IN_CH, HEADS, OUT_CH, E = (50000, 256, 4, 64, 25000)
        key = jax.random.key(seed)
        k1, k2, k3, k4, k5 = jax.random.split(key, 5)
        x = jax.random.normal(k1, (N, IN_CH), dtype=jnp.float32)
        edge_index = jax.random.randint(k2, (2, E), 0, N, dtype=jnp.int64)
        bw = float(np.sqrt(6.0 / (IN_CH + HEADS * OUT_CH)))
        ba = float(np.sqrt(6.0 / (HEADS + OUT_CH)))
        weight = jax.random.uniform(k3, (IN_CH, HEADS * OUT_CH), jnp.float32, -bw, bw)
        attn_l = jax.random.uniform(k4, (HEADS, OUT_CH), jnp.float32, -ba, ba)
        attn_r = jax.random.uniform(k5, (HEADS, OUT_CH), jnp.float32, -ba, ba)
        return {'x': x, 'edge_index': edge_index, 'weight': weight, 'attn_l': attn_l, 'attn_r': attn_r}
    _L3_gnn_all = _L3_gnn_setup()
    _L3_gnn_in = {k: v for k, v in _L3_gnn_all.items() if k in ('weight', 'attn_l', 'attn_r')}
    del _L3_gnn_all
    return {'x': x, 'src': src, 'dst': dst, 'L0_gnn_W_in': _L0_gnn_in['W_in'], 'L0_gnn_b_in': _L0_gnn_in['b_in'], 'L0_gnn_W_out': _L0_gnn_in['W_out'], 'L0_gnn_b_out': _L0_gnn_in['b_out'], 'L1_gnn_W0': _L1_gnn_in['W0'], 'L1_gnn_att_src0': _L1_gnn_in['att_src0'], 'L1_gnn_att_dst0': _L1_gnn_in['att_dst0'], 'L1_gnn_b0': _L1_gnn_in['b0'], 'L1_gnn_W1': _L1_gnn_in['W1'], 'L1_gnn_att_src1': _L1_gnn_in['att_src1'], 'L1_gnn_att_dst1': _L1_gnn_in['att_dst1'], 'L1_gnn_b1': _L1_gnn_in['b1'], 'L2_gnn_W': _L2_gnn_in['W'], 'L2_gnn_att_src': _L2_gnn_in['att_src'], 'L2_gnn_att_dst': _L2_gnn_in['att_dst'], 'L2_gnn_bias': _L2_gnn_in['bias'], 'L3_gnn_weight': _L3_gnn_in['weight'], 'L3_gnn_attn_l': _L3_gnn_in['attn_l'], 'L3_gnn_attn_r': _L3_gnn_in['attn_r']}

def reference(x, src, dst, L0_gnn_W_in, L0_gnn_b_in, L0_gnn_W_out, L0_gnn_b_out, L1_gnn_W0, L1_gnn_att_src0, L1_gnn_att_dst0, L1_gnn_b0, L1_gnn_W1, L1_gnn_att_src1, L1_gnn_att_dst1, L1_gnn_b1, L2_gnn_W, L2_gnn_att_src, L2_gnn_att_dst, L2_gnn_bias, L3_gnn_weight, L3_gnn_attn_l, L3_gnn_attn_r):
    import jax
    import jax.numpy as jnp

    def _L0_gnn_ref(h, src, dst, W_in, b_in, W_out, b_out):
        import jax, jax.numpy as jnp
        import numpy as np
        N_NODES = 50000
        N_EDGES = 25000
        D_IN = 256
        D_HID = 256
        D_OUT = 256
        GAMMA = 0.0
        K_STEPS = 6

        def _spmm(h, src, dst, inv_deg):
            msg = h[src]
            agg = jax.ops.segment_sum(msg, dst, num_segments=h.shape[0])
            return agg * inv_deg[:, None]

        def _linear_diffusion(h, src, dst, gamma=GAMMA, k=K_STEPS):
            n = h.shape[0]
            deg = jax.ops.segment_sum(jnp.ones((src.shape[0],), h.dtype), dst, num_segments=n)
            inv_deg = 1.0 / jnp.clip(deg, 1.0)
            out = h
            term = h
            for i in range(1, k + 1):
                term = (_spmm(term, src, dst, inv_deg) + gamma * term) / float(i)
                out = out + term
            return out
        x = h @ W_in.T + b_in
        x = jax.nn.silu(x)
        x = _linear_diffusion(x, src, dst)
        x = x @ W_out.T + b_out
        return x

    def _L1_gnn_ref(x, edge_index, W0, att_src0, att_dst0, b0, W1, att_src1, att_dst1, b1):
        import jax, jax.numpy as jnp
        import numpy as np
        N = 50000
        E = 25000
        D_IN = 256
        HID = 32
        HEADS = 8
        D_OUT = 64
        NEG_SLOPE = 0.2

        def _gat_conv(x, src, dst, W, att_src, att_dst, bias, heads, out_dim, concat):
            n = x.shape[0]
            h = (x @ W.T).reshape(n, heads, out_dim)
            a_s = jnp.sum(h * att_src, axis=-1)
            a_d = jnp.sum(h * att_dst, axis=-1)
            logits = jax.nn.leaky_relu(a_s[src] + a_d[dst], NEG_SLOPE)
            m = jax.ops.segment_max(logits, dst, num_segments=n)
            e = jnp.exp(logits - m[dst])
            den = jax.ops.segment_sum(e, dst, num_segments=n)
            alpha = e / (den[dst] + 1e-16)
            out = jax.ops.segment_sum(alpha[:, :, None] * h[src], dst, num_segments=n)
            out = out.reshape(n, heads * out_dim) if concat else out.mean(axis=1)
            return out + bias
        n = x.shape[0]
        loop = jnp.arange(n, dtype=edge_index.dtype)
        ei = jnp.concatenate([edge_index, jnp.stack([loop, loop])], axis=1)
        src, dst = (ei[0], ei[1])
        out1 = jax.nn.elu(_gat_conv(x, src, dst, W0, att_src0, att_dst0, b0, HEADS, HID, True))
        _ = _gat_conv(out1, src, dst, W1, att_src1, att_dst1, b1, 1, D_OUT, False)
        return out1

    def _L2_gnn_ref(x, edge_index, W, att_src, att_dst, bias):
        import jax, jax.numpy as jnp
        import numpy as np
        N = 50000
        E = 25000
        HEADS = 4
        C = 64
        IN = 256
        NEG_SLOPE = 0.2

        def _gat_forward(x, edge_index, W, att_src, att_dst, bias):
            n = x.shape[0]
            h = (x @ W).reshape(n, HEADS, C)
            loop = jnp.arange(n, dtype=edge_index.dtype)
            src = jnp.concatenate([edge_index[0], loop])
            dst = jnp.concatenate([edge_index[1], loop])
            a_src = jnp.einsum('nhc,hc->nh', h, att_src)
            a_dst = jnp.einsum('nhc,hc->nh', h, att_dst)
            logits = a_src[src] + a_dst[dst]
            logits = jnp.where(logits >= 0, logits, NEG_SLOPE * logits)
            seg_max = jax.ops.segment_max(logits, dst, num_segments=n)
            seg_max = jnp.where(jnp.isfinite(seg_max), seg_max, 0.0)
            ex = jnp.exp(logits - seg_max[dst])
            denom = jax.ops.segment_sum(ex, dst, num_segments=n)
            alpha = ex / (denom[dst] + 1e-16)
            msgs = alpha[:, :, None] * h[src]
            out = jax.ops.segment_sum(msgs, dst, num_segments=n)
            out = out.reshape(n, HEADS * C) + bias
            return jax.nn.relu(out)
        return _gat_forward(x, edge_index, W, att_src, att_dst, bias)

    def _L3_gnn_ref(x, edge_index, weight, attn_l, attn_r):
        import jax, jax.numpy as jnp
        import numpy as np
        N, IN_CH, HEADS, OUT_CH, E = (50000, 256, 4, 64, 25000)
        heads, out_ch = attn_l.shape
        n = x.shape[0]
        xt = jnp.matmul(x, weight).reshape(-1, heads, out_ch)
        row, col = (edge_index[0], edge_index[1])
        alpha_l = jnp.einsum('ehd,hd->eh', xt[row], attn_l)
        alpha_r = jnp.einsum('ehd,hd->eh', xt[col], attn_r)
        alpha = jax.nn.softmax(jax.nn.leaky_relu(alpha_l + alpha_r, 0.01), axis=1)
        tmp = jnp.einsum('nh,nhd->nd', alpha[:n], xt[col[:n]])
        out = jnp.broadcast_to(tmp[:, None, :], (n, heads, out_ch))
        return out.reshape(n, heads * out_ch)
    edge_index = jnp.stack([src, dst])
    x = _layernorm(x + _L0_gnn_ref(x, src, dst, L0_gnn_W_in, L0_gnn_b_in, L0_gnn_W_out, L0_gnn_b_out), axis=-1)
    x = _layernorm(x + _L1_gnn_ref(x, edge_index, L1_gnn_W0, L1_gnn_att_src0, L1_gnn_att_dst0, L1_gnn_b0, L1_gnn_W1, L1_gnn_att_src1, L1_gnn_att_dst1, L1_gnn_b1), axis=-1)
    x = _layernorm(x + _L2_gnn_ref(x, edge_index, L2_gnn_W, L2_gnn_att_src, L2_gnn_att_dst, L2_gnn_bias), axis=-1)
    x = _layernorm(x + _L3_gnn_ref(x, edge_index, L3_gnn_weight, L3_gnn_attn_l, L3_gnn_attn_r), axis=-1)
    return x

_drawn_inputs = setup_inputs


def setup_inputs(seed=0):
    import zlib

    import numpy as np

    out = dict(_drawn_inputs(seed))
    spreads = {'L1_gnn_b0': (0.0, 0.1), 'L1_gnn_b1': (0.0, 0.1)}
    factors = {'L2_gnn_bias': 3.713}
    for name, (base, spread) in spreads.items():
        noise = np.random.default_rng([zlib.crc32(name.encode()), seed]).standard_normal(out[name].shape)
        drawn = base * np.exp(spread * noise) if base else spread * noise
        out[name] = jnp.asarray(drawn.astype(out[name].dtype))
    for name, factor in factors.items():
        out[name] = (out[name] * factor).astype(out[name].dtype)
    return out
```

```python
import concourse.bass as bass
from concourse import mybir
from contextlib import ExitStack

F32 = mybir.dt.float32
I32 = mybir.dt.int32
ALU = mybir.AluOpType
ACT = mybir.ActivationFunctionType
AX = mybir.AxisListType
DVE_ENGINE = mybir.EngineType.DVE
PE_ENGINE = mybir.EngineType.PE

N, D, E = 3125, 256, 50000
P = 128
NT = -(-N // P)
NPAD = NT * P
NLAST = N - (NT - 1) * P
ET = -(-E // P)
STEPS = ET + NT - 1
HALF = 4
PAIRS = -(-STEPS // (2 * HALF))
GROUPS = 2 * PAIRS
TABLE = (GROUPS + 1) * HALF
TG = -(-ET // P)
PADF = 4096.0
RUN = -(-E // P)
RUNPAD = -(-RUN // 8) * 8
RLAST = E - (P - 1) * RUN
MAXH = 8
SW = D + 2 * MAXH
KSTEPS = 6
BIG = 3.0e38
EPS_LN = 1e-5
CH = 5


def gnn_kernel(nc, x_in, src_in, dst_in, win, b_in, wout, b_out, w0, as0, ad0, b0,
               w2, as2, ad2, b2, w3, al3, ar3, out):
    ctx = ExitStack()
    with ctx:
        def sb(name, shape, dt=F32):
            return ctx.enter_context(nc.sbuf_tensor(name, shape, dt))

        def pb(name, shape, dt=F32):
            return ctx.enter_context(nc.psum_tensor(name, shape, dt))

        phase_sems = []

        def sem(name):
            s = nc.alloc_semaphore(name=name)
            phase_sems.append(s)
            return s

        def end_phase():
            nc.clear_and_free_semaphores(phase_sems)
            nc.all_engine_barrier()
            phase_sems.clear()

        def dram(name, shape, dt=F32):
            return nc.dram_tensor(name, shape, dt, kind="Internal").ap()

        t_term = dram("t_term", (NPAD, D))
        t_h1 = dram("t_h1", (NPAD, D + 8))
        t_h2 = dram("t_h2", (NPAD, D + 4))
        t_h3 = dram("t_h3", (NPAD, D + 4))
        t_as1 = dram("t_as1", (NPAD, 8))
        t_as2 = dram("t_as2", (NPAD, 4))
        t_al3 = dram("t_al3", (NPAD, 4))
        t_mx1 = dram("t_mx1", (P * RUN, 8))
        t_mx2 = dram("t_mx2", (P * RUN, 4))

        def rows(t):
            return t.rearrange("(b p) d -> p b d", p=P)

        x = sb("x", [P, NT, D])
        feat = sb("feat", [P, NT * SW])
        acc = sb("acc", [P, NT * SW])
        total = sb("total", [P, NT, D])
        tmp = sb("tmp", [P, NT * D])
        feat3 = feat[:, :].rearrange("p (b w) -> p b w", w=SW)
        acc3 = acc[:, :].rearrange("p (b w) -> p b w", w=SW)
        tmp3 = tmp[:, :].rearrange("p (b d) -> p b d", d=D)
        weights = sb("weights", [P, 5, 2, D])
        wraw = sb("wraw", [P, 3, 2, D])
        bias = sb("bias", [P, 4, D])
        att = sb("att", [P, 6, D])
        msg = sb("msg", [P, 2 * HALF, SW])
        onehot = sb("onehot", [P, 2, HALF, P])
        onehot_t = sb("onehot_t", [P, 2, HALF, P])
        z = sb("z", [P, 2, HALF, MAXH])
        node_ad = sb("node_ad", [P, NT * 2 * MAXH])
        node_ad3 = node_ad[:, :].rearrange("p (b w) -> p b w", w=2 * MAXH)
        wself = sb("wself", [P, NT, MAXH])
        mx = sb("mx", [P, NT, MAXH])
        idx_ring = sb("idx_ring", [P, 2 * HALF], I32)
        small_ring = sb("small_ring", [P, 2, HALF * MAXH])
        step_src = sb("step_src", [P, TABLE], I32)
        step_dst = sb("step_dst", [P, TABLE])
        step_tile = sb("step_tile", [1, TABLE], I32)
        run_src = sb("run_src", [P, RUNPAD], I32)
        run_cut = sb("run_cut", [P, RUN])
        head_src = sb("head_src", [P, NT], I32)
        head_dst = sb("head_dst", [P, NT], I32)
        last_edge = sb("last_edge", [P, NT], I32)
        no_edge = sb("no_edge", [P, NT])
        deg = sb("deg", [P, NT])
        invdeg = sb("invdeg", [P, NT])
        stat = sb("stat", [P, 4, NT])
        kinv = sb("kinv", [P, KSTEPS])
        ident = sb("ident", [P, P])
        ones = sb("ones", [P, P])
        lower = sb("lower", [P, P])
        iota_n = sb("iota_n", [P, P])
        carry = sb("carry", [P, 4, P])

        psum_a = pb("psum_a", [P, 4, 512])
        psum_t = pb("psum_t", [P, 2, 512])
        psum_e = pb("psum_e", [P, 2, 512])

        acc_i = acc[:, :].bitcast(I32)
        tmp_i = tmp[:, :].bitcast(I32)
        raw_i = acc_i[:, 0:2 * TG * P].rearrange("p (k g e) -> p k g e", k=2, g=TG)
        raw_f = acc[:, 1024:1024 + 2 * TG * P].rearrange("p (k g e) -> p k g e", k=2, g=TG)
        SPAD = NT - 1 + TG * P + P
        src_t = acc[:, 2048:2048 + SPAD]
        dst_t = acc[:, 2048 + SPAD:2048 + 2 * SPAD]
        thr = acc[:, 4096:4096 + NT - 1]
        cmp = acc[:, 4200:4200 + (NT - 1) * TG].rearrange("p (b g) -> p b g", g=TG)
        cnt = acc[:, 4400:4400 + NT - 1]
        first_step = acc[:, 4450:4450 + NT - 1]
        bnum = acc[:, 4500:4500 + NT]
        bstep = tmp[:, 0:TABLE]
        siota = tmp[:, 512:512 + TABLE]
        hit = tmp[:, 1024:1024 + TABLE]
        fsrc = tmp[:, 1536:1536 + TABLE]
        iota_i = tmp_i[:, 2048:2048 + 512]
        cur_i = tmp_i[:, 2560:2560 + RUN]
        prev_i = tmp_i[:, 3072:3072 + RUN]

        rows_loaded = sem("rows_loaded")
        runs_loaded = sem("runs_loaded")
        x_loaded = sem("x_loaded")
        w_loaded = sem("w_loaded")
        v_loaded = sem("v_loaded")
        pads_set = sem("pads_set")
        consts_set = sem("consts_set")
        pool_step = sem("pool_step")
        setup_chain = sem("setup_chain")
        rows_float = sem("rows_float")
        rows_turned = sem("rows_turned")
        counted = sem("counted")
        cnt_summed = sem("cnt_summed")
        w_turned = sem("w_turned")
        w_copied = sem("w_copied")
        tables_ready = sem("tables_ready")

        with nc.Block() as block:
            @block.sync
            def _(sp):
                sp.wait_ge(pads_set, 5)
                for k, a in enumerate((src_in, dst_in)):
                    full = (TG - 1) * P
                    sp.dma_start(raw_i[:, k, 0:TG - 1, :],
                                 a[0:full * P].rearrange("(g p e) -> p g e", p=P, e=P)).then_inc(rows_loaded, 16)
                    r = E // P - full
                    sp.dma_start(raw_i[0:r, k, TG - 1, :],
                                 a[full * P:(full + r) * P].rearrange("(p e) -> p e", e=P)).then_inc(rows_loaded, 16)
                    sp.dma_start(raw_i[r:r + 1, k, TG - 1, 0:E % P],
                                 a[E - E % P:E].rearrange("(p e) -> p e", p=1)).then_inc(rows_loaded, 16)
                whole = (P - 1) * RUN
                for dest, a, shift in ((run_src, src_in, 0), (cur_i, dst_in, 0)):
                    sp.dma_start(dest[0:P - 1, 0:RUN],
                                 a[0:whole].rearrange("(p e) -> p e", e=RUN)).then_inc(runs_loaded, 16)
                    sp.dma_start(dest[P - 1:P, 0:RLAST],
                                 a[whole:E].rearrange("(p e) -> p e", p=1)).then_inc(runs_loaded, 16)
                sp.dma_start(prev_i[0:1, 1:RUN], dst_in[0:RUN - 1].rearrange("(p e) -> p e", p=1)).then_inc(runs_loaded, 16)
                sp.dma_start(prev_i[1:P - 1, :], dst_in[RUN - 1:whole - 1].rearrange("(p e) -> p e", e=RUN)).then_inc(runs_loaded, 16)
                sp.dma_start(prev_i[P - 1:P, 0:RLAST], dst_in[whole - 1:E - 1].rearrange("(p e) -> p e", p=1)).then_inc(runs_loaded, 16)

            @block.scalar
            def _(act):
                act.dma_start(wraw[:, 0, :, :], win.rearrange("(k p) n -> p k n", p=P)).then_inc(w_loaded, 16)
                act.dma_start(wraw[:, 1, :, :], wout.rearrange("(k p) n -> p k n", p=P)).then_inc(w_loaded, 16)
                act.dma_start(wraw[:, 2, :, :], w0.rearrange("(k p) n -> p k n", p=P)).then_inc(w_loaded, 16)
                act.wait_ge(pads_set, 5)
                act.dma_start(x[:, 0:NT - 1, :], x_in[0:(NT - 1) * P, :].rearrange("(b p) d -> p b d", p=P)).then_inc(x_loaded, 16)
                act.dma_start(x[0:NLAST, NT - 1, :], x_in[(NT - 1) * P:N, :]).then_inc(x_loaded, 16)
                act.dma_start(weights[:, 3, :, :], w2.rearrange("(k p) n -> p k n", p=P)).then_inc(v_loaded, 16)
                act.dma_start(weights[:, 4, :, :], w3.rearrange("(k p) n -> p k n", p=P)).then_inc(v_loaded, 16)
                for k, a in enumerate((b_in, b_out, b0, b2)):
                    act.dma_start(bias[:, k, :], a.rearrange("(a n) -> a n", a=1).to_broadcast([P, D])).then_inc(v_loaded, 16)
                for k, a in enumerate((as0, ad0, as2, ad2, al3, ar3)):
                    act.dma_start(att[:, k, :], a.rearrange("(a n) -> a n", a=1).to_broadcast([P, D])).then_inc(v_loaded, 16)
                act.wait_ge(x_loaded, 32)
                act.wait_ge(v_loaded, 192)
                for w in range(3):
                    act.wait_ge(w_turned, w + 1)
                    nc.scalar.copy(weights[:, w, :, :], psum_a[:, w, :].rearrange("p (k n) -> p k n", k=2)).then_inc(w_copied, 1)

            @block.gpsimd
            def _(pool):
                nc.gpsimd.memset(raw_i[:, 0, :, :], 0).then_inc(pads_set, 1)
                nc.gpsimd.memset(raw_i[:, 1, :, :], int(PADF)).then_inc(pads_set, 1)
                nc.gpsimd.memset(x[:, NT - 1, :], 0.0).then_inc(pads_set, 1)
                nc.gpsimd.memset(run_src[:, :], 0).then_inc(pads_set, 1)
                nc.gpsimd.memset(tmp_i[:, 2560:3072 + RUN], -1).then_inc(pads_set, 1)
                nc.gpsimd.memset(ident[:, :], 0.0).then_inc(pool_step, 1)
                nc.gpsimd.memset(lower[:, :], 1.0).then_inc(pool_step, 1)
                nc.gpsimd.memset(ones[:, :], 1.0).then_inc(pool_step, 1)
                nc.gpsimd.memset(acc[:, 2048:2048 + 2 * SPAD], 0.0).then_inc(pool_step, 1)
                nc.gpsimd.iota(iota_i, pattern=[[1, 512]], base=0, channel_multiplier=0).then_inc(pool_step, 1)
                pool.wait_ge(pool_step, 5)
                nc.gpsimd.affine_select(out=ident[:, :], in_=ident[:, :], compare_op=ALU.not_equal, fill=1.0,
                                        base=0, pattern=[[-1, P]], channel_multiplier=1).then_inc(consts_set, 1)
                nc.gpsimd.affine_select(out=lower[:, :], in_=lower[:, :], compare_op=ALU.is_ge, fill=0.0,
                                        base=0, pattern=[[1, P]], channel_multiplier=-1).then_inc(consts_set, 1)
                for s in range(2 * HALF):
                    nc.gpsimd.memset(msg[:, s, D:D + 1], 1.0).then_inc(consts_set, 1)

            @block.tensor
            def _(pe):
                pe.wait_ge(consts_set, 10)
                pe.wait_ge(w_loaded, 48)
                for w in range(3):
                    for k in range(2):
                        for j in range(2):
                            last = nc.tensor.transpose(psum_a[:, w, k * D + j * P:k * D + (j + 1) * P],
                                                       wraw[:, w, j, k * P:(k + 1) * P], ident[:, :])
                    last.then_inc(w_turned, 1)
                pe.wait_ge(rows_float, 1)
                for k in range(2):
                    for g in range(TG):
                        last = nc.tensor.transpose(psum_t[:, k, g * P:(g + 1) * P], raw_f[:, k, g, :], ident[:, :])
                    last.then_inc(rows_turned, 1)
                pe.wait_ge(counted, 1)
                nc.tensor.matmul(psum_e[:, 0, 0:NT - 1], ones[:, :], cnt, start=True, stop=True).then_inc(cnt_summed, 1)

            @block.vector
            def _(dve):
                done = [0]

                def link(ins):
                    done[0] += 1
                    ins.then_inc(setup_chain, 1)
                    dve.wait_ge(setup_chain, done[0])

                V = nc.vector
                dve.wait_ge(pool_step, 5)
                link(V.tensor_copy(siota, iota_i[:, 0:TABLE]))
                link(V.tensor_copy(iota_n[:, :], siota[:, 0:P]))
                link(V.tensor_scalar(kinv[:, :], siota[:, 0:KSTEPS], 1.0, None, ALU.add))
                link(V.reciprocal(kinv[:, :], kinv[:, :]))
                link(V.tensor_copy(bnum, siota[:, 0:NT]))
                link(V.tensor_scalar(thr, siota[:, 1:NT], float(P), None, ALU.mult))
                dve.wait_ge(rows_loaded, 96)
                V.tensor_copy(raw_f[:, 0, :, :], raw_i[:, 0, :, :])
                link(V.tensor_copy(raw_f[:, 1, :, :], raw_i[:, 1, :, :]))
                nc.vector.tensor_scalar(hit[:, 0:1], bnum[:, 0:1], 1.0, None, ALU.mult).then_inc(rows_float, 1)
                link(V.tensor_tensor(cmp, raw_f[:, 1, :, P - 1].unsqueeze(1).to_broadcast([P, NT - 1, TG]),
                                     thr.unsqueeze(2).to_broadcast([P, NT - 1, TG]), ALU.is_lt))
                V.tensor_reduce(cnt, cmp, AX.X, ALU.add).then_inc(counted, 1)
                dve.wait_ge(cnt_summed, 1)
                link(V.tensor_tensor(first_step, psum_e[:, 0, 0:NT - 1], bnum[:, 1:NT], ALU.add))
                link(V.memset(bstep, 0.0))
                for b in range(NT - 1):
                    link(V.scalar_tensor_tensor(out=bstep, in0=siota, scalar=first_step[:, b:b + 1], in1=bstep,
                                                op0=ALU.is_ge, op1=ALU.add))
                link(V.tensor_copy(step_tile[0:1, :], bstep[0:1, :]))
                dve.wait_ge(rows_turned, 2)
                V.tensor_copy(src_t[:, NT - 1:NT - 1 + TG * P], psum_t[:, 0, :])
                V.memset(dst_t[:, NT - 1 + TG * P:SPAD], PADF)
                link(V.tensor_copy(dst_t[:, NT - 1:NT - 1 + TG * P], psum_t[:, 1, :]))
                V.tensor_copy(head_src[:, :], psum_t[:, 0, 0:NT])
                V.tensor_copy(head_dst[:, :], psum_t[:, 1, 0:NT])
                V.memset(fsrc, 0.0)
                link(V.tensor_scalar(step_dst[:, :], bstep, -float(P), None, ALU.mult))
                for b in range(NT):
                    lo = NT - 1 - b
                    for table, sink in ((src_t, fsrc), (dst_t, step_dst[:, :])):
                        link(V.scalar_tensor_tensor(out=hit, in0=bstep, scalar=float(b), in1=table[:, lo:lo + TABLE],
                                                    op0=ALU.is_equal, op1=ALU.mult))
                        link(V.tensor_tensor(sink, sink, hit, ALU.add))
                link(V.tensor_copy(step_src[:, :], fsrc))
                dve.wait_ge(runs_loaded, 112)
                link(V.tensor_tensor(run_cut[:, :], cur_i, prev_i, ALU.not_equal))
                link(V.tensor_scalar(run_cut[:, :], run_cut[:, :], -BIG, None, ALU.mult))
                V.memset(acc[:, 0:16], 0.0).then_inc(tables_ready, 1)
                dve.wait_ge(tables_ready, 1)

        def project(name, source, w):
            staged = sem(name + "_staged")
            turned = sem(name + "_turned")
            copied = sem(name + "_copied")
            product = sem(name + "_product")
            stored = sem(name + "_stored")
            gate = sem(name + "_gate")
            stage = acc[:, 0:CH * D]
            xt = acc[:, CH * D:2 * CH * D]
            turn = psum_t[:, :, :].rearrange("p a b -> p (a b)")
            prod = psum_a[:, :, :].rearrange("p a b -> p (a b)")[:, 0:CH * D]
            src_flat = source[:, :, :].rearrange("p b d -> p (b d)")
            turn_e = psum_e[:, 0, 0:D]
            with nc.Block() as block:
                @block.scalar
                def _(act):
                    with act.Fori(0, NT // CH) as c:
                        nc.scalar.copy(stage, src_flat[:, bass.ds(c * (CH * D), CH * D)]).then_inc(staged, 1)
                        act.wait_ge(turned, c + 1)
                        nc.scalar.copy(xt[:, 0:4 * D], turn).then_inc(copied, 1)
                        nc.scalar.copy(xt[:, 4 * D:5 * D], turn_e).then_inc(copied, 1)
                        act.wait_ge(product, c + 1)
                        act.sem_inc(gate, 1)
                        for t in range(CH):
                            nc.scalar.copy(feat[:, bass.ds(c * (CH * SW) + t * SW, D)],
                                           prod[:, t * D:(t + 1) * D]).then_inc(stored, 1)

                @block.tensor
                def _(pe):
                    with pe.Fori(0, NT // CH) as c:
                        pe.wait_ge(staged, c + 1)
                        for t in range(CH):
                            for k in range(2):
                                at = (2 * t + k) * P
                                o = turn[:, at:at + P] if t < 4 else turn_e[:, at - 8 * P:at - 7 * P]
                                last = nc.tensor.transpose(o, stage[:, at:at + P], ident[:, :])
                        last.then_inc(turned, 1)
                        pe.wait_ge(copied, c * 2 + 2)
                        for t in range(CH):
                            for k in range(2):
                                last = nc.tensor.matmul(prod[:, t * D:(t + 1) * D], xt[:, (2 * t + k) * P:(2 * t + k + 1) * P],
                                                        weights[:, w, k, :], start=(k == 0), stop=(k == 1))
                        last.then_inc(product, 1)
                        pe.wait_ge(stored, c * CH + CH)

        def edge_pass(name, table, heads, passes):
            width = D + heads if heads else D
            W = D + heads if heads else D + 1
            fetched = [sem(f"{name}_fetched{s}") for s in range(2 * HALF)]
            idx_copied = sem(name + "_e_idx_copied")
            gate = sem(name + "_e_gate")
            oh_ready = sem(name + "_e_oh_ready")
            t_done = sem(name + "_e_t_done")
            oht_ready = sem(name + "_e_oht_ready")
            ex_done = sem(name + "_e_ex_done")
            z_ready = sem(name + "_e_z_ready")
            w_ready = sem(name + "_e_w_ready")
            wm_ready = sem(name + "_e_wm_ready")
            agg_done = sem(name + "_e_agg_done")
            acc_done = sem(name + "_e_acc_done")
            chain = sem(name + "_e_chain")
            term_ready = sem(name + "_e_term_ready")
            table_ready = sem(name + "_e_table_ready")
            acc_clear = sem(name + "_e_acc_clear")
            total_added = sem(name + "_e_total_added")
            NSTEP = GROUPS * HALF
            why = "the tables are built with tiles in this range"

            def tile_of(engine, g, k):
                return nc.values_load(step_tile[0:1, bass.ds(g * HALF + k, 1)], engines=(engine,),
                                      min_val=0, max_val=NT - 1, skip_runtime_bounds_check_because=why)

            def loop_passes(eng, body):
                if passes == 1:
                    body(0)
                else:
                    with eng.Fori(0, passes) as r:
                        body(r)

            with nc.Block() as block:
                if not heads:
                    @block.sync
                    def _(sp):
                        def one(r):
                            sp.wait_ge(term_ready, r + 1)
                            sp.dma_start(rows(table), feat3[:, :, 0:D]).then_inc(table_ready, 16)
                        loop_passes(sp, one)
                        sp.wait_ge(table_ready, 16 * passes)

                @block.gpsimd
                def _(pool):
                    def one(r):
                        def group(i, a, first):
                            g = 2 * i + a
                            if not first:
                                pool.wait_ge(agg_done, r * NSTEP + (g - 1) * HALF)
                                pool.sem_inc(gate, 1)
                            nc.gpsimd.tensor_copy(idx_ring[:, a * HALF:(a + 1) * HALF],
                                                  step_src[:, bass.ds(g * HALF, HALF)]).then_inc(idx_copied, 1)
                            pool.wait_ge(idx_copied, r * GROUPS + g + 1)
                            pool.sem_inc(gate, 1)
                            for k in range(HALF):
                                s = a * HALF + k
                                pool.indirect_dma_start(
                                    out=msg[:, s, 0:width], out_offset=None, in_=table[:, :],
                                    in_offset=bass.IndirectOffsetOnAxis(ap=idx_ring[:, s:s + 1], axis=0)
                                ).then_inc(fetched[s], 16)
                        for a in range(2):
                            group(0, a, True)
                        with pool.Fori(1, PAIRS) as i:
                            for a in range(2):
                                group(i, a, False)
                        if passes > 1:
                            pool.wait_ge(table_ready, r * 16 + 16)
                    loop_passes(pool, one)

                @block.tensor
                def _(pe):
                    def one(r):
                        def turn(g, b):
                            pe.wait_ge(oh_ready, r * (GROUPS + 1) + g + 1)
                            for k in range(HALF):
                                last = nc.tensor.transpose(psum_t[:, b, k * P:(k + 1) * P], onehot[:, b, k, :], ident[:, :])
                            last.then_inc(t_done, 1)

                        def expand(g, b):
                            pe.wait_ge(oht_ready, g + 1)
                            for k in range(HALF):
                                tile = tile_of(PE_ENGINE, g, k)
                                last = nc.tensor.matmul(psum_e[:, b, k * 16:(k + 1) * 16], onehot_t[:, b, k, :],
                                                        node_ad[:, bass.ds(tile * 16, 16)], start=True, stop=True)
                            last.then_inc(ex_done, 1)

                        def group(i, a, first):
                            g = 2 * i + a
                            if heads:
                                if not (first and a == 0):
                                    pe.wait_ge(oht_ready, g)
                                turn(g + 1, 1 - a)
                                pe.wait_ge(wm_ready, g + 1)
                            else:
                                pe.wait_ge(oh_ready, r * (GROUPS + 1) + g + 1)
                            for k in range(HALF):
                                s = a * HALF + k
                                if not heads:
                                    pe.wait_ge(fetched[s], (r * PAIRS + i + 1) * 16)
                                if not (first and a == 0):
                                    pe.wait_ge(acc_done, r * NSTEP + (g - 1) * HALF + k + 1)
                                nc.tensor.matmul(psum_a[:, k, 0:W], onehot[:, a, k, :], msg[:, s, 0:W],
                                                 start=True, stop=True).then_inc(agg_done, 1)
                            if heads:
                                if not (first and a == 0):
                                    pe.wait_ge(z_ready, g)
                                expand(g + 1, 1 - a)

                        if heads:
                            turn(0, 0)
                            expand(0, 0)
                        elif passes > 1:
                            pe.wait_ge(acc_clear, r + 1)
                        for a in range(2):
                            group(0, a, True)
                        with pe.Fori(1, PAIRS) as i:
                            for a in range(2):
                                group(i, a, False)
                    loop_passes(pe, one)

                if heads:
                    @block.scalar
                    def _(act):
                        def copy_turned(g, b):
                            act.wait_ge(t_done, g + 1)
                            nc.scalar.copy(onehot_t[:, b, :, :].rearrange("p k e -> p (k e)"),
                                           psum_t[:, b, :]).then_inc(oht_ready, 1)

                        def group(i, a, first):
                            g = 2 * i + a
                            act.wait_ge(z_ready, g + 1)
                            nc.scalar.activation(msg[:, a * HALF:(a + 1) * HALF, D:D + heads], z[:, a, :, 0:heads],
                                                 ACT.Exp).then_inc(w_ready, 1)
                            if not (first and a == 0):
                                act.wait_ge(ex_done, g)
                            copy_turned(g + 1, 1 - a)

                        copy_turned(0, 0)
                        for a in range(2):
                            group(0, a, True)
                        with act.Fori(1, PAIRS) as i:
                            for a in range(2):
                                group(i, a, False)

                @block.vector
                def _(dve):
                    V = nc.vector
                    ZCH = 3

                    def one(r):
                        def make_onehot(g, b, k):
                            ins = V.tensor_scalar(onehot[:, b, k, :], iota_n[:, :], step_dst[:, bass.ds(g * HALF + k, 1)],
                                                  None, ALU.is_equal)
                            if k == HALF - 1:
                                ins.then_inc(oh_ready, 1)

                        def add_step(g, k, tile, nothing_before=False):
                            if not nothing_before:
                                dve.wait_ge(acc_done, r * NSTEP + g * HALF + k)
                            dve.wait_ge(agg_done, r * NSTEP + g * HALF + k + 1)
                            at = acc[:, bass.ds(tile * SW, W)]
                            V.tensor_tensor(at, at, psum_a[:, k, 0:W], ALU.add).then_inc(acc_done, 1)

                        def scores(g, i, a):
                            for k in range(HALF):
                                dve.wait_ge(fetched[a * HALF + k], (i + 1) * 16)
                            dve.wait_ge(ex_done, g + 1)
                            ex = psum_e[:, a, 0:HALF * 16].rearrange("p (k w) -> p k w", w=16)
                            zz = z[:, a, :, 0:heads]
                            V.tensor_tensor(zz, msg[:, a * HALF:(a + 1) * HALF, D:D + heads],
                                            ex[:, :, 0:heads], ALU.add).then_inc(chain, 1)
                            dve.wait_ge(chain, g * ZCH + 1)
                            V.scalar_tensor_tensor(out=zz, in0=zz, scalar=0.2, in1=zz,
                                                   op0=ALU.mult, op1=ALU.max).then_inc(chain, 1)
                            dve.wait_ge(chain, g * ZCH + 2)
                            V.tensor_tensor(zz, zz, ex[:, :, 8:8 + heads], ALU.subtract).then_inc(chain, 1)
                            dve.wait_ge(chain, g * ZCH + 3)
                            V.tensor_scalar(zz, zz, 0.0, None, ALU.min).then_inc(z_ready, 1)

                        def weigh(g, a):
                            dve.wait_ge(w_ready, g + 1)
                            m = msg[:, a * HALF:(a + 1) * HALF, 0:D].rearrange("p k (h c) -> p k h c", h=heads)
                            w = msg[:, a * HALF:(a + 1) * HALF, D:D + heads].unsqueeze(3).to_broadcast(
                                [P, HALF, heads, D // heads])
                            V.tensor_tensor(m, m, w, ALU.mult).then_inc(wm_ready, 1)

                        def group(i, a, first):
                            g = 2 * i + a
                            adds = not (first and a == 0)
                            if adds:
                                tiles = [tile_of(DVE_ENGINE, g - 1, k) for k in range(HALF)]
                            if heads:
                                scores(g, i, a)
                            for k in range(HALF):
                                if adds:
                                    add_step(g - 1, k, tiles[k], first and k == 0)
                                make_onehot(g + 1, 1 - a, k)
                            if heads:
                                weigh(g, a)

                        if passes > 1:
                            V.memset(acc[:, :], 0.0).then_inc(acc_clear, 1)
                            dve.wait_ge(acc_clear, r + 1)
                        for k in range(HALF):
                            make_onehot(0, 0, k)
                        for a in range(2):
                            group(0, a, True)
                        with dve.Fori(1, PAIRS) as i:
                            for a in range(2):
                                group(i, a, False)
                        tiles = [tile_of(DVE_ENGINE, GROUPS - 1, k) for k in range(HALF)]
                        for k in range(HALF):
                            add_step(GROUPS - 1, k, tiles[k])
                        dve.wait_ge(acc_done, r * NSTEP + NSTEP)
                        if heads:
                            return
                        ECH = 4
                        V.tensor_copy(deg[:, :], acc3[:, :, D]).then_inc(chain, 1)
                        dve.wait_ge(chain, r * ECH + 1)
                        V.tensor_scalar(invdeg[:, :], deg[:, :], 1.0, None, ALU.max).then_inc(chain, 1)
                        dve.wait_ge(chain, r * ECH + 2)
                        V.reciprocal(invdeg[:, :], invdeg[:, :]).then_inc(chain, 1)
                        dve.wait_ge(chain, r * ECH + 3)
                        V.tensor_scalar(invdeg[:, :], invdeg[:, :], kinv[:, bass.ds(r, 1)], None, ALU.mult).then_inc(chain, 1)
                        dve.wait_ge(chain, r * ECH + 4)
                        V.tensor_tensor(feat3[:, :, 0:D], acc3[:, :, 0:D],
                                        invdeg[:, :].unsqueeze(2).to_broadcast([P, NT, D]), ALU.mult).then_inc(term_ready, 1)
                        dve.wait_ge(term_ready, r + 1)
                        V.tensor_tensor(total[:, :, :], total[:, :, :], feat3[:, :, 0:D], ALU.add).then_inc(total_added, 1)
                        dve.wait_ge(table_ready, r * 16 + 16)
                        dve.wait_ge(total_added, r + 1)
                    loop_passes(dve, one)

        end_phase()
        project("in", x, 0)
        end_phase()
        c0 = sem("c0")
        e0_ready = sem("e0_ready")
        e0_done = sem("e0_done")
        h0_ready = sem("h0_ready")
        h0_stored = sem("h0_stored")
        with nc.Block() as block:
            @block.vector
            def _(dve):
                V = nc.vector
                V.tensor_tensor(feat3[:, :, 0:D], feat3[:, :, 0:D],
                                bias[:, 0, :].unsqueeze(1).to_broadcast([P, NT, D]), ALU.add).then_inc(e0_ready, 1)
                dve.wait_ge(e0_done, 1)
                V.tensor_scalar(tmp[:, :], tmp[:, :], 1.0, None, ALU.add).then_inc(c0, 1)
                dve.wait_ge(c0, 1)
                V.reciprocal(tmp[:, :], tmp[:, :]).then_inc(c0, 1)
                dve.wait_ge(c0, 2)
                V.tensor_tensor(total[:, :, :], feat3[:, :, 0:D], tmp3, ALU.mult).then_inc(h0_ready, 1)

            @block.scalar
            def _(act):
                act.wait_ge(e0_ready, 1)
                nc.scalar.activation(tmp3, feat3[:, :, 0:D], ACT.Exp, scale=-1.0).then_inc(e0_done, 1)

            @block.sync
            def _(sp):
                sp.wait_ge(h0_ready, 1)
                sp.dma_start(rows(t_term), total[:, :, :]).then_inc(h0_stored, 16)
                sp.wait_ge(h0_stored, 16)
        end_phase()

        edge_pass("diffuse", t_term, 0, KSTEPS)
        end_phase()

        def norm_steps(link, ask_act, y):
            V = nc.vector
            link(V.tensor_reduce(stat[:, 0, :], y, AX.X, ALU.add))
            link(V.tensor_scalar(stat[:, 1, :], stat[:, 0, :], 1.0 / D, None, ALU.mult))
            ask_act(V.tensor_tensor(y, y, stat[:, 1, :].unsqueeze(2).to_broadcast([P, NT, D]), ALU.subtract))
            link(V.tensor_reduce(stat[:, 2, :], tmp3, AX.X, ALU.add))
            ask_act(V.tensor_scalar(stat[:, 3, :], stat[:, 2, :], 1.0 / D, EPS_LN, ALU.mult, ALU.add))
            link(V.reciprocal(stat[:, 0, :], stat[:, 3, :]))
            link(V.tensor_tensor(x[:, :, :], y, stat[:, 0, :].unsqueeze(2).to_broadcast([P, NT, D]), ALU.mult))

        def finish(name, kind, nh=0, bias_row=0):
            chain = sem(name + "_chain")
            asked = sem(name + "_asked")
            answered = sem(name + "_answered")
            stored = sem(name + "_stored")
            with nc.Block() as block:
                @block.vector
                def _(dve):
                    V = nc.vector
                    n = [0, 0]

                    def link(ins):
                        n[0] += 1
                        ins.then_inc(chain, 1)
                        dve.wait_ge(chain, n[0])

                    def ask_act(ins):
                        n[1] += 1
                        ins.then_inc(asked, 1)
                        dve.wait_ge(answered, n[1])

                    y = total[:, :, :]
                    if kind == "linear":
                        link(V.tensor_tensor(y, feat3[:, :, 0:D], bias[:, 1, :].unsqueeze(1).to_broadcast([P, NT, D]), ALU.add))
                    elif kind in ("elu", "relu"):
                        link(V.tensor_scalar(mx[:, :, 0:nh], acc3[:, :, D:D + nh], 1e-16, None, ALU.add))
                        link(V.reciprocal(mx[:, :, 0:nh], mx[:, :, 0:nh]))
                        for h in range(nh):
                            c = D // nh
                            V.tensor_tensor(y[:, :, h * c:(h + 1) * c], acc3[:, :, h * c:(h + 1) * c],
                                            mx[:, :, h:h + 1].to_broadcast([P, NT, c]), ALU.mult).then_inc(chain, 1)
                        n[0] += nh
                        dve.wait_ge(chain, n[0])
                        link(V.tensor_tensor(y, y, bias[:, bias_row, :].unsqueeze(1).to_broadcast([P, NT, D]), ALU.add))
                        if kind == "elu":
                            ask_act(V.tensor_scalar(tmp3, y, 0.0, None, ALU.min))
                            link(V.scalar_tensor_tensor(out=y, in0=y, scalar=0.0, in1=tmp3, op0=ALU.max, op1=ALU.add))
                            link(V.tensor_scalar(y, y, -1.0, None, ALU.add))
                        else:
                            link(V.tensor_scalar(y, y, 0.0, None, ALU.max))
                    else:
                        zz = mx[:, :, 0:nh]
                        c = D // nh
                        link(V.tensor_tensor(zz, zz, acc3[:, :, D:D + nh], ALU.add))
                        link(V.scalar_tensor_tensor(out=zz, in0=zz, scalar=0.01, in1=zz, op0=ALU.mult, op1=ALU.max))
                        link(V.tensor_reduce(stat[:, 0, :], zz, AX.X, ALU.max))
                        ask_act(V.tensor_tensor(zz, zz, stat[:, 0, :].unsqueeze(2).to_broadcast([P, NT, nh]), ALU.subtract))
                        link(V.tensor_reduce(stat[:, 1, :], zz, AX.X, ALU.add))
                        link(V.reciprocal(stat[:, 1, :], stat[:, 1, :]))
                        link(V.tensor_tensor(zz, zz, stat[:, 1, :].unsqueeze(2).to_broadcast([P, NT, nh]), ALU.mult))
                        for h in range(nh):
                            V.tensor_tensor(tmp3[:, :, h * c:(h + 1) * c], acc3[:, :, h * c:(h + 1) * c],
                                            mx[:, :, h:h + 1].to_broadcast([P, NT, c]), ALU.mult).then_inc(chain, 1)
                        n[0] += nh
                        dve.wait_ge(chain, n[0])
                        link(V.tensor_tensor(tmp3[:, :, 0:2 * c], tmp3[:, :, 0:2 * c], tmp3[:, :, 2 * c:4 * c], ALU.add))
                        link(V.tensor_tensor(tmp3[:, :, 0:c], tmp3[:, :, 0:c], tmp3[:, :, c:2 * c], ALU.add))
                        link(V.tensor_tensor(y.rearrange("p b (h c) -> p b h c", h=nh),
                                             x[:, :, :].rearrange("p b (h c) -> p b h c", h=nh),
                                             tmp3[:, :, 0:c].unsqueeze(2).to_broadcast([P, NT, nh, c]), ALU.add))
                    if kind != "edges":
                        link(V.tensor_tensor(y, y, x[:, :, :], ALU.add))
                    norm_steps(link, ask_act, y)
                    V.memset(stat[:, 1, :], 0.0).then_inc(asked, 1)

                @block.scalar
                def _(act):
                    k = 0
                    if kind == "elu":
                        k += 1
                        act.wait_ge(asked, k)
                        nc.scalar.activation(tmp3, tmp3, ACT.Exp).then_inc(answered, 1)
                    if kind == "edges":
                        k += 1
                        act.wait_ge(asked, k)
                        nc.scalar.activation(mx[:, :, 0:nh], mx[:, :, 0:nh], ACT.Exp).then_inc(answered, 1)
                    act.wait_ge(asked, k + 1)
                    nc.scalar.activation(tmp3, total[:, :, :], ACT.Square).then_inc(answered, 1)
                    act.wait_ge(asked, k + 2)
                    nc.scalar.activation(stat[:, 3, :], stat[:, 3, :], ACT.Sqrt).then_inc(answered, 1)
                    if kind == "edges":
                        act.wait_ge(asked, k + 3)
                        act.dma_start(out[0:(NT - 1) * P, :].rearrange("(b p) d -> p b d", p=P), x[:, 0:NT - 1, :]).then_inc(stored, 16)
                        act.dma_start(out[(NT - 1) * P:N, :], x[0:NLAST, NT - 1, :]).then_inc(stored, 16)
                        act.wait_ge(stored, 32)

        def coefficients(name, nh, att_s, att_d, t_feat, t_score, right_in_table=False):
            chain = sem(name + "_cf_chain")
            ready = sem(name + "_cf_ready")
            stored = sem(name + "_cf_stored")
            c = D // nh
            src_score = mx[:, :, 0:nh]
            dst_score = node_ad3[:, :, 0:nh]
            with nc.Block() as block:
                @block.vector
                def _(dve):
                    V = nc.vector
                    n = [0]

                    def link(ins):
                        n[0] += 1
                        ins.then_inc(chain, 1)
                        dve.wait_ge(chain, n[0])
                    for row, sink in ((att_s, src_score), (att_d, dst_score)):
                        link(V.tensor_tensor(tmp3, feat3[:, :, 0:D], att[:, row, :].unsqueeze(1).to_broadcast([P, NT, D]), ALU.mult))
                        link(V.tensor_reduce(sink, tmp3.rearrange("p b (h c) -> p b h c", h=nh), AX.X, ALU.add))
                    V.tensor_copy(feat3[:, :, D:D + nh], dst_score if right_in_table else src_score).then_inc(ready, 1)

                @block.sync
                def _(sp):
                    sp.wait_ge(ready, 1)
                    sp.dma_start(rows(t_feat), feat3[:, :, 0:D + nh]).then_inc(stored, 16)
                    sp.dma_start(rows(t_score), mx[:, :, 0:nh]).then_inc(stored, 16)
                    sp.wait_ge(stored, 32)

        def maxima(name, nh, t_score, t_mx):
            fetched = [sem(f"{name}_mf{s}") for s in range(2 * HALF)]
            idx_copied = sem(name + "_m_idx")
            gate = sem(name + "_m_gate")
            gate_dve = sem(name + "_m_gate_dve")
            moved = sem(name + "_m_moved")
            chain = sem(name + "_m_chain")
            scanned = sem(name + "_m_scanned")
            turned = sem(name + "_m_turned")
            carried = sem(name + "_m_carried")
            back = sem(name + "_m_back")
            scores_ready = sem(name + "_m_ready")
            stored = sem(name + "_m_stored")
            got = sem(name + "_m_got")
            asked = sem(name + "_m_asked")
            answered = sem(name + "_m_answered")
            edge_s = tmp[:, 0:RUNPAD * nh]
            scan_s = tmp[:, RUNPAD * MAXH:RUNPAD * MAXH + RUN * nh]
            edge3 = edge_s.rearrange("p (j h) -> p j h", h=nh)
            scan3 = scan_s.rearrange("p (j h) -> p j h", h=nh)
            src_score = feat3[:, :, D:D + nh]
            node_mx = mx[:, :, 0:nh]
            with nc.Block() as block:
                @block.gpsimd
                def _(pool):
                    def group(i, a, first):
                        g = 2 * i + a
                        if not first:
                            pool.wait_ge(moved, g - 1)
                            pool.sem_inc(gate, 1)
                        nc.gpsimd.tensor_copy(idx_ring[:, a * HALF:(a + 1) * HALF],
                                              run_src[:, bass.ds(g * HALF, HALF)]).then_inc(idx_copied, 1)
                        pool.wait_ge(idx_copied, g + 1)
                        pool.sem_inc(gate, 1)
                        for k in range(HALF):
                            s = a * HALF + k
                            pool.indirect_dma_start(
                                out=small_ring[:, a, k * nh:(k + 1) * nh], out_offset=None, in_=t_score[:, :],
                                in_offset=bass.IndirectOffsetOnAxis(ap=idx_ring[:, s:s + 1], axis=0)
                            ).then_inc(fetched[s], 16)
                    for a in range(2):
                        group(0, a, True)
                    with pool.Fori(1, RUNPAD // (2 * HALF)) as i:
                        for a in range(2):
                            group(i, a, False)
                    pool.wait_ge(stored, 16)
                    for b in range(NT):
                        pool.indirect_dma_start(
                            out=mx[:, b, 0:nh], out_offset=None, in_=t_mx[:, :],
                            in_offset=bass.IndirectOffsetOnAxis(ap=last_edge[:, b:b + 1], axis=0)).then_inc(got, 16)

                @block.sync
                def _(sp):
                    sp.wait_ge(scores_ready, 1)
                    sp.dma_start(t_mx.rearrange("(p j) h -> p (j h)", p=P), scan_s).then_inc(stored, 16)
                    sp.wait_ge(stored, 16)

                @block.tensor
                def _(pe):
                    pe.wait_ge(scanned, 1)
                    nc.tensor.transpose(psum_e[0:nh, 0, 0:P], carry[:, 0, 0:nh], ident[:, :])
                    nc.tensor.transpose(psum_e[0:nh, 1, 0:P], carry[:, 1, 0:nh], ident[:, :]).then_inc(turned, 1)
                    pe.wait_ge(carried, 1)
                    nc.tensor.transpose(psum_a[:, 0, 0:nh], carry[0:nh, 2, 0:P], ident[0:nh, 0:nh]).then_inc(back, 1)

                @block.scalar
                def _(act):
                    act.wait_ge(asked, 1)
                    nc.scalar.activation(wself[:, :, 0:nh], wself[:, :, 0:nh], ACT.Exp).then_inc(answered, 1)

                @block.vector
                def _(dve):
                    V = nc.vector
                    n = [0]

                    def link(ins):
                        n[0] += 1
                        ins.then_inc(chain, 1)
                        dve.wait_ge(chain, n[0])

                    with dve.Fori(0, RUNPAD // (2 * HALF)) as i:
                        for a in range(2):
                            for k in range(HALF):
                                dve.wait_ge(fetched[a * HALF + k], i * 16 + 16)
                            dve.sem_inc(gate_dve, 1)
                            V.tensor_copy(edge_s[:, bass.ds((2 * i + a) * (HALF * nh), HALF * nh)],
                                          small_ring[:, a, 0:HALF * nh]).then_inc(moved, 1)
                    dve.wait_ge(moved, RUNPAD // HALF)
                    for h in range(nh):
                        V.tensor_tensor_scan(scan3[:, :, h], run_cut[:, :], edge3[:, 0:RUN, h], -BIG,
                                             ALU.add, ALU.max).then_inc(chain, 1)
                    n[0] += nh
                    dve.wait_ge(chain, n[0])
                    link(V.tensor_reduce(stat[:, 0, 0:1], run_cut[:, :], AX.X, ALU.min))
                    link(V.tensor_copy(carry[:, 0, 0:nh], scan3[:, RUN - 1, :]))
                    V.tensor_copy(carry[:, 1, 0:nh], stat[:, 0, 0:1].to_broadcast([P, nh])).then_inc(scanned, 1)
                    dve.wait_ge(turned, 1)
                    link(V.tensor_copy(carry[0:nh, 3, 0:P], psum_e[0:nh, 1, 0:P]))
                    link(V.memset(carry[0:nh, 2, 0:1], -BIG))
                    V.tensor_tensor_scan(carry[0:nh, 2, 1:P], carry[0:nh, 3, 0:P - 1], psum_e[0:nh, 0, 0:P - 1], -BIG,
                                         ALU.add, ALU.max).then_inc(carried, 1)
                    dve.wait_ge(back, 1)
                    link(V.tensor_copy(stat[:, 1, 0:nh], psum_a[:, 0, 0:nh]))
                    for h in range(nh):
                        V.tensor_tensor_scan(scan3[:, :, h], run_cut[:, :], edge3[:, 0:RUN, h], stat[:, 1, h:h + 1],
                                             ALU.add, ALU.max).then_inc(chain, 1)
                    n[0] += nh
                    dve.wait_ge(chain, n[0])
                    V.memset(stat[:, 2, :], 0.0).then_inc(scores_ready, 1)
                    link(V.tensor_tensor(wself[:, :, 0:nh], src_score, node_ad3[:, :, 0:nh], ALU.add))
                    link(V.scalar_tensor_tensor(out=wself[:, :, 0:nh], in0=wself[:, :, 0:nh], scalar=0.2,
                                                in1=wself[:, :, 0:nh], op0=ALU.mult, op1=ALU.max))
                    dve.wait_ge(got, NT * 16)
                    link(V.tensor_tensor(node_mx, node_mx, no_edge[:, :].unsqueeze(2).to_broadcast([P, NT, nh]), ALU.min))
                    link(V.tensor_tensor(node_mx, node_mx, src_score, ALU.max))
                    link(V.tensor_tensor(node_mx, node_mx, node_ad3[:, :, 0:nh], ALU.add))
                    link(V.scalar_tensor_tensor(out=node_ad3[:, :, 8:8 + nh], in0=node_mx, scalar=0.2, in1=node_mx,
                                                op0=ALU.mult, op1=ALU.max))
                    V.tensor_tensor(wself[:, :, 0:nh], wself[:, :, 0:nh], node_ad3[:, :, 8:8 + nh], ALU.subtract).then_inc(asked, 1)
                    dve.wait_ge(answered, 1)
                    c = D // nh
                    for h in range(nh):
                        V.tensor_tensor(acc3[:, :, h * c:(h + 1) * c], feat3[:, :, h * c:(h + 1) * c],
                                        wself[:, :, h:h + 1].to_broadcast([P, NT, c]), ALU.mult).then_inc(chain, 1)
                    n[0] += nh
                    link(V.tensor_copy(acc3[:, :, D:D + nh], wself[:, :, 0:nh]))

        def last_edges():
            chain = sem("le_chain")
            summed = sem("le_summed")
            with nc.Block() as block:
                @block.tensor
                def _(pe):
                    nc.tensor.matmul(psum_a[:, 0, 0:NT], lower[:, :], deg[:, :], start=True, stop=True).then_inc(summed, 1)
                    nc.tensor.matmul(psum_a[:, 1, 0:NT], ones[:, :], deg[:, :], start=True, stop=True).then_inc(summed, 1)

                @block.vector
                def _(dve):
                    V = nc.vector
                    n = [0]

                    def link(ins):
                        n[0] += 1
                        ins.then_inc(chain, 1)
                        dve.wait_ge(chain, n[0])
                    dve.wait_ge(summed, 2)
                    link(V.memset(stat[:, 1, :], 0.0))
                    link(V.tensor_copy(stat[:, 3, :], psum_a[:, 1, 0:NT]))
                    link(V.tensor_tensor_scan(stat[:, 0, :], stat[:, 3, :], stat[:, 1, :], 0.0, ALU.add, ALU.add))
                    link(V.tensor_tensor(stat[:, 0, :], stat[:, 0, :], stat[:, 3, :], ALU.subtract))
                    link(V.tensor_tensor(stat[:, 0, :], stat[:, 0, :], psum_a[:, 0, 0:NT], ALU.add))
                    link(V.tensor_scalar(stat[:, 0, :], stat[:, 0, :], -1.0, 0.0, ALU.add, ALU.max))
                    link(V.tensor_copy(last_edge[:, :], stat[:, 0, :]))
                    link(V.tensor_scalar(no_edge[:, :], deg[:, :], 0.0, None, ALU.is_gt))
                    link(V.tensor_scalar(no_edge[:, :], no_edge[:, :], 2.0, -1.0, ALU.mult, ALU.add))
                    link(V.tensor_scalar(no_edge[:, :], no_edge[:, :], BIG, None, ALU.mult))

        project("out", total, 1)
        end_phase()
        finish("norm0", "linear")
        end_phase()
        last_edges()
        end_phase()

        project("gat1", x, 2)
        end_phase()
        coefficients("gat1", 8, 0, 1, t_h1, t_as1)
        end_phase()
        maxima("gat1", 8, t_as1, t_mx1)
        end_phase()
        edge_pass("gat1", t_h1, 8, 1)
        end_phase()
        finish("norm1", "elu", 8, 2)
        end_phase()

        project("gat2", x, 3)
        end_phase()
        coefficients("gat2", 4, 2, 3, t_h2, t_as2)
        end_phase()
        maxima("gat2", 4, t_as2, t_mx2)
        end_phase()
        edge_pass("gat2", t_h2, 4, 1)
        end_phase()
        finish("norm2", "relu", 4, 3)
        end_phase()

        project("top", x, 4)
        end_phase()
        coefficients("top", 4, 4, 5, t_h3, t_al3, right_in_table=True)
        end_phase()
        top_got = sem("top_got")
        with nc.Block() as block:
            @block.gpsimd
            def _(pool):
                for b in range(NT):
                    pool.indirect_dma_start(out=acc3[:, b, 0:D + 4], out_offset=None, in_=t_h3[:, :],
                                            in_offset=bass.IndirectOffsetOnAxis(ap=head_dst[:, b:b + 1], axis=0)).then_inc(top_got, 16)
                    pool.indirect_dma_start(out=mx[:, b, 0:4], out_offset=None, in_=t_al3[:, :],
                                            in_offset=bass.IndirectOffsetOnAxis(ap=head_src[:, b:b + 1], axis=0)).then_inc(top_got, 16)
                pool.wait_ge(top_got, 2 * NT * 16)
        end_phase()
        finish("norm3", "edges", 4)
        end_phase()


_INS = ['x', 'src', 'dst', 'L0_gnn_W_in', 'L0_gnn_b_in', 'L0_gnn_W_out', 'L0_gnn_b_out', 'L1_gnn_W0',
        'L1_gnn_att_src0', 'L1_gnn_att_dst0', 'L1_gnn_b0', 'L2_gnn_W', 'L2_gnn_att_src', 'L2_gnn_att_dst',
        'L2_gnn_bias', 'L3_gnn_weight', 'L3_gnn_attn_l', 'L3_gnn_attn_r']


def kernel(**inputs):
    import numpy as _np
    import concourse.bacc as _bacc
    from concourse import mybir as _mybir
    from concourse.bass_utils import run_bass_kernel_spmd as _run

    nc = _bacc.Bacc("TRN2", target_bir_lowering=False, num_devices=1)
    arrays, args = {}, []
    for name in _INS:
        a = _np.ascontiguousarray(inputs[name])
        if "att" in name:
            a = a.reshape(-1)
        arrays[f"in_{name}"] = a
        args.append(nc.dram_tensor(f"in_{name}", a.shape, _mybir.dt.from_np(a.dtype), kind="ExternalInput").ap())
    out = nc.dram_tensor("out", (3125, 256), _mybir.dt.float32, kind="ExternalOutput").ap()
    gnn_kernel(nc, *args, out)
    r = _run(nc, [arrays], core_ids=[0])
    return r.results[0]["out"]
```

```python
import concourse.bass as bass
from concourse import mybir
from contextlib import ExitStack

F32 = mybir.dt.float32
I32 = mybir.dt.int32
BF16 = mybir.dt.bfloat16
ALU = mybir.AluOpType
ACT = mybir.ActivationFunctionType
AX = mybir.AxisListType
DVE_ENGINE = mybir.EngineType.DVE
PE_ENGINE = mybir.EngineType.PE

N, D, E = 3125, 256, 50000
P = 128
NT = -(-N // P)
NPAD = NT * P
NLAST = N - (NT - 1) * P
ET = -(-E // P)
STEPS = ET + NT - 1
HALF = 4
RING = 8
OHR = 4
AHEAD = 3
TURNS = -(-STEPS // (RING * HALF))
GROUPS = RING * TURNS
TABLE = (GROUPS + RING) * HALF
TG = -(-ET // P)
PADF = 4096.0
RUN = -(-E // P)
RUNPAD = -(-RUN // 8) * 8
PTURNS = 4
MAXPC = 34
RLAST = E - (P - 1) * RUN
MAXH = 8
SW = D + 2 * MAXH
KSTEPS = 6
BIG = 3.0e38
EPS_LN = 1e-5
CH = 5


def gnn_kernel(nc, x_in, src_in, dst_in, win, b_in, wout, b_out, w0, as0, ad0, b0,
               w2, as2, ad2, b2, w3, al3, ar3, out):
    ctx = ExitStack()
    with ctx:
        def sb(name, shape, dt=F32):
            return ctx.enter_context(nc.sbuf_tensor(name, shape, dt))

        def pb(name, shape, dt=F32):
            return ctx.enter_context(nc.psum_tensor(name, shape, dt))

        phase_sems = []

        def sem(name):
            s = nc.alloc_semaphore(name=name)
            phase_sems.append(s)
            return s

        def end_phase():
            nc.clear_and_free_semaphores(phase_sems)
            nc.all_engine_barrier()
            phase_sems.clear()

        def dram(name, shape, dt=F32):
            return nc.dram_tensor(name, shape, dt, kind="Internal").ap()

        t_term = dram("t_term", (NPAD, D))
        t_h1 = dram("t_h1", (NPAD, D + 8))
        t_h2 = dram("t_h2", (NPAD, D + 4))
        t_h3 = dram("t_h3", (NPAD, D + 4))
        t_as1 = dram("t_as1", (NPAD, 8))
        t_as2 = dram("t_as2", (NPAD, 4))
        t_al3 = dram("t_al3", (NPAD, 4))
        t_mx1 = dram("t_mx1", (P * RUN, 8))
        t_mx2 = dram("t_mx2", (P * RUN, 4))

        def rows(t):
            return t.rearrange("(b p) d -> p b d", p=P)

        x = sb("x", [P, NT, D])
        feat = sb("feat", [P, NT * SW])
        acc = sb("acc", [P, NT * SW])
        total = sb("total", [P, NT, D])
        feat3 = feat[:, :].rearrange("p (b w) -> p b w", w=SW)
        acc3 = acc[:, :].rearrange("p (b w) -> p b w", w=SW)
        weights = sb("weights", [P, 5, 2, D])
        wraw = sb("wraw", [P, 3, 2, D])
        bias = sb("bias", [P, 4, D])
        att = sb("att", [P, 6, D])
        msg_flat = sb("msg_flat", [P, RING * HALF * SW])
        msg = msg_flat[:, :].rearrange("p (s w) -> p s w", w=SW)
        tmp = msg_flat[:, 0:NT * D]
        tmp3 = tmp.rearrange("p (b d) -> p b d", d=D)
        onehot = sb("onehot", [P, OHR, HALF, P])
        onehot_t = sb("onehot_t", [P, 2, HALF, P])
        onehot_tb = onehot_t[:, :, :, :].rearrange("p s k e -> p s (k e)").bitcast(BF16)
        z = sb("z", [P, 2, HALF, MAXH])
        node_ad = sb("node_ad", [P, NT * 2 * MAXH])
        node_ad3 = node_ad[:, :].rearrange("p (b w) -> p b w", w=2 * MAXH)
        score_tab_b = sb("score_tab_b", [P, 3, NT * MAXH], BF16)
        wself = sb("wself", [P, NT, MAXH])
        mx = sb("mx", [P, NT, MAXH])
        idx_ring = sb("idx_ring", [P, max(RING * HALF, MAXPC)], I32)
        score_tab = sb("score_tab", [P, NT * MAXH])
        run_place = sb("run_place", [P, RUNPAD])
        run_tile = sb("run_tile", [P, RUNPAD])
        small_ring = sb("small_ring", [P, MAXPC * MAXH])
        step_src = sb("step_src", [P, TABLE], I32)
        step_dst = sb("step_dst", [P, TABLE])
        step_tile = sb("step_tile", [1, TABLE], I32)
        run_src = sb("run_src", [P, RUNPAD], I32)
        run_cut = sb("run_cut", [P, RUN])
        head_src = sb("head_src", [P, NT], I32)
        head_dst = sb("head_dst", [P, NT], I32)
        last_edge = sb("last_edge", [P, NT], I32)
        no_edge = sb("no_edge", [P, NT])
        deg = sb("deg", [P, NT])
        invdeg = sb("invdeg", [P, NT])
        stat = sb("stat", [P, 4, NT])
        kinv = sb("kinv", [P, KSTEPS])
        ident = sb("ident", [P, P])
        ident_b = sb("ident_b", [P, P], BF16)
        ones = sb("ones", [P, P])
        lower = sb("lower", [P, P])
        iota_n = sb("iota_n", [P, P])
        carry = sb("carry", [P, 4, P])

        psum_a = pb("psum_a", [P, 4, 512])
        psum_t = pb("psum_t", [P, 2, 512])
        psum_tb = psum_t[:, :, :].bitcast(BF16)
        psum_e = pb("psum_e", [P, 2, 512])

        acc_i = acc[:, :].bitcast(I32)
        tmp_i = tmp.bitcast(I32)
        raw_i = acc_i[:, 0:2 * TG * P].rearrange("p (k g e) -> p k g e", k=2, g=TG)
        raw_f = acc[:, 1024:1024 + 2 * TG * P].rearrange("p (k g e) -> p k g e", k=2, g=TG)
        SPAD = NT - 1 + TG * P + P
        src_t = acc[:, 2048:2048 + SPAD]
        dst_t = acc[:, 2048 + SPAD:2048 + 2 * SPAD]
        thr = acc[:, 4096:4096 + NT - 1]
        cmp = acc[:, 4200:4200 + (NT - 1) * TG].rearrange("p (b g) -> p b g", g=TG)
        cnt = acc[:, 4400:4400 + NT - 1]
        first_step = acc[:, 4450:4450 + NT - 1]
        bnum = acc[:, 4500:4500 + NT]
        bstep = tmp[:, 0:TABLE]
        siota = tmp[:, 512:512 + TABLE]
        hit = tmp[:, 1024:1024 + TABLE]
        fsrc = tmp[:, 1536:1536 + TABLE]
        iota_i = tmp_i[:, 2048:2048 + 512]
        cur_i = tmp_i[:, 2560:2560 + RUN]
        prev_i = tmp_i[:, 3072:3072 + RUN]
        part_i = tmp_i[:, 3584:3584 + RUNPAD]

        rows_loaded = sem("rows_loaded")
        runs_loaded = sem("runs_loaded")
        x_loaded = sem("x_loaded")
        w_loaded = sem("w_loaded")
        v_loaded = sem("v_loaded")
        pads_set = sem("pads_set")
        consts_set = sem("consts_set")
        pool_step = sem("pool_step")
        setup_chain = sem("setup_chain")
        rows_float = sem("rows_float")
        rows_turned = sem("rows_turned")
        counted = sem("counted")
        cnt_summed = sem("cnt_summed")
        w_turned = sem("w_turned")
        w_copied = sem("w_copied")
        tables_ready = sem("tables_ready")

        with nc.Block() as block:
            @block.sync
            def _(sp):
                sp.wait_ge(pads_set, 5)
                for k, a in enumerate((src_in, dst_in)):
                    full = (TG - 1) * P
                    sp.dma_start(raw_i[:, k, 0:TG - 1, :],
                                 a[0:full * P].rearrange("(g p e) -> p g e", p=P, e=P)).then_inc(rows_loaded, 16)
                    r = E // P - full
                    sp.dma_start(raw_i[0:r, k, TG - 1, :],
                                 a[full * P:(full + r) * P].rearrange("(p e) -> p e", e=P)).then_inc(rows_loaded, 16)
                    sp.dma_start(raw_i[r:r + 1, k, TG - 1, 0:E % P],
                                 a[E - E % P:E].rearrange("(p e) -> p e", p=1)).then_inc(rows_loaded, 16)
                whole = (P - 1) * RUN
                for dest, a, shift in ((run_src, src_in, 0), (cur_i, dst_in, 0)):
                    sp.dma_start(dest[0:P - 1, 0:RUN],
                                 a[0:whole].rearrange("(p e) -> p e", e=RUN)).then_inc(runs_loaded, 16)
                    sp.dma_start(dest[P - 1:P, 0:RLAST],
                                 a[whole:E].rearrange("(p e) -> p e", p=1)).then_inc(runs_loaded, 16)
                sp.dma_start(prev_i[0:1, 1:RUN], dst_in[0:RUN - 1].rearrange("(p e) -> p e", p=1)).then_inc(runs_loaded, 16)
                sp.dma_start(prev_i[1:P - 1, :], dst_in[RUN - 1:whole - 1].rearrange("(p e) -> p e", e=RUN)).then_inc(runs_loaded, 16)
                sp.dma_start(prev_i[P - 1:P, 0:RLAST], dst_in[whole - 1:E - 1].rearrange("(p e) -> p e", p=1)).then_inc(runs_loaded, 16)

            @block.scalar
            def _(act):
                act.dma_start(wraw[:, 0, :, :], win.rearrange("(k p) n -> p k n", p=P)).then_inc(w_loaded, 16)
                act.dma_start(wraw[:, 1, :, :], wout.rearrange("(k p) n -> p k n", p=P)).then_inc(w_loaded, 16)
                act.dma_start(wraw[:, 2, :, :], w0.rearrange("(k p) n -> p k n", p=P)).then_inc(w_loaded, 16)
                act.wait_ge(pads_set, 5)
                act.dma_start(x[:, 0:NT - 1, :], x_in[0:(NT - 1) * P, :].rearrange("(b p) d -> p b d", p=P)).then_inc(x_loaded, 16)
                act.dma_start(x[0:NLAST, NT - 1, :], x_in[(NT - 1) * P:N, :]).then_inc(x_loaded, 16)
                act.dma_start(weights[:, 3, :, :], w2.rearrange("(k p) n -> p k n", p=P)).then_inc(v_loaded, 16)
                act.dma_start(weights[:, 4, :, :], w3.rearrange("(k p) n -> p k n", p=P)).then_inc(v_loaded, 16)
                for k, a in enumerate((b_in, b_out, b0, b2)):
                    act.dma_start(bias[:, k, :], a.rearrange("(a n) -> a n", a=1).to_broadcast([P, D])).then_inc(v_loaded, 16)
                for k, a in enumerate((as0, ad0, as2, ad2, al3, ar3)):
                    act.dma_start(att[:, k, :], a.rearrange("(a n) -> a n", a=1).to_broadcast([P, D])).then_inc(v_loaded, 16)
                act.wait_ge(x_loaded, 32)
                act.wait_ge(v_loaded, 192)
                for w in range(3):
                    act.wait_ge(w_turned, w + 1)
                    nc.scalar.copy(weights[:, w, :, :], psum_a[:, w, :].rearrange("p (k n) -> p k n", k=2)).then_inc(w_copied, 1)

            @block.gpsimd
            def _(pool):
                nc.gpsimd.memset(raw_i[:, 0, :, :], 0).then_inc(pads_set, 1)
                nc.gpsimd.memset(raw_i[:, 1, :, :], int(PADF)).then_inc(pads_set, 1)
                nc.gpsimd.memset(x[:, NT - 1, :], 0.0).then_inc(pads_set, 1)
                nc.gpsimd.memset(run_src[:, :], 0).then_inc(pads_set, 1)
                nc.gpsimd.memset(tmp_i[:, 2560:3072 + RUN], -1).then_inc(pads_set, 1)
                nc.gpsimd.memset(ident[:, :], 0.0).then_inc(pool_step, 1)
                nc.gpsimd.memset(lower[:, :], 1.0).then_inc(pool_step, 1)
                nc.gpsimd.memset(ones[:, :], 1.0).then_inc(pool_step, 1)
                nc.gpsimd.memset(acc[:, 2048:2048 + 2 * SPAD], 0.0).then_inc(pool_step, 1)
                nc.gpsimd.iota(iota_i, pattern=[[1, 512]], base=0, channel_multiplier=0).then_inc(pool_step, 1)
                pool.wait_ge(pool_step, 5)
                nc.gpsimd.affine_select(out=ident[:, :], in_=ident[:, :], compare_op=ALU.not_equal, fill=1.0,
                                        base=0, pattern=[[-1, P]], channel_multiplier=1).then_inc(consts_set, 1)
                nc.gpsimd.affine_select(out=lower[:, :], in_=lower[:, :], compare_op=ALU.is_ge, fill=0.0,
                                        base=0, pattern=[[1, P]], channel_multiplier=-1).then_inc(consts_set, 1)

            @block.tensor
            def _(pe):
                pe.wait_ge(consts_set, 2)
                pe.wait_ge(w_loaded, 48)
                for w in range(3):
                    for k in range(2):
                        for j in range(2):
                            last = nc.tensor.transpose(psum_a[:, w, k * D + j * P:k * D + (j + 1) * P],
                                                       wraw[:, w, j, k * P:(k + 1) * P], ident[:, :])
                    last.then_inc(w_turned, 1)
                pe.wait_ge(rows_float, 1)
                for k in range(2):
                    for g in range(TG):
                        last = nc.tensor.transpose(psum_t[:, k, g * P:(g + 1) * P], raw_f[:, k, g, :], ident[:, :])
                    last.then_inc(rows_turned, 1)
                pe.wait_ge(counted, 1)
                nc.tensor.matmul(psum_e[:, 0, 0:NT - 1], ones[:, :], cnt, start=True, stop=True).then_inc(cnt_summed, 1)

            @block.vector
            def _(dve):
                done = [0]

                def link(ins):
                    done[0] += 1
                    ins.then_inc(setup_chain, 1)
                    dve.wait_ge(setup_chain, done[0])

                V = nc.vector
                dve.wait_ge(pool_step, 5)
                link(V.tensor_copy(siota, iota_i[:, 0:TABLE]))
                link(V.tensor_copy(iota_n[:, :], siota[:, 0:P]))
                link(V.tensor_scalar(kinv[:, :], siota[:, 0:KSTEPS], 1.0, None, ALU.add))
                link(V.reciprocal(kinv[:, :], kinv[:, :]))
                link(V.tensor_copy(bnum, siota[:, 0:NT]))
                dve.wait_ge(consts_set, 2)
                link(V.tensor_copy(ident_b[:, :], ident[:, :]))
                link(V.tensor_scalar(thr, siota[:, 1:NT], float(P), None, ALU.mult))
                dve.wait_ge(rows_loaded, 96)
                V.tensor_copy(raw_f[:, 0, :, :], raw_i[:, 0, :, :])
                link(V.tensor_copy(raw_f[:, 1, :, :], raw_i[:, 1, :, :]))
                nc.vector.tensor_scalar(hit[:, 0:1], bnum[:, 0:1], 1.0, None, ALU.mult).then_inc(rows_float, 1)
                link(V.tensor_tensor(cmp, raw_f[:, 1, :, P - 1].unsqueeze(1).to_broadcast([P, NT - 1, TG]),
                                     thr.unsqueeze(2).to_broadcast([P, NT - 1, TG]), ALU.is_lt))
                V.tensor_reduce(cnt, cmp, AX.X, ALU.add).then_inc(counted, 1)
                dve.wait_ge(cnt_summed, 1)
                link(V.tensor_tensor(first_step, psum_e[:, 0, 0:NT - 1], bnum[:, 1:NT], ALU.add))
                link(V.memset(bstep, 0.0))
                for b in range(NT - 1):
                    link(V.scalar_tensor_tensor(out=bstep, in0=siota, scalar=first_step[:, b:b + 1], in1=bstep,
                                                op0=ALU.is_ge, op1=ALU.add))
                link(V.tensor_copy(step_tile[0:1, :], bstep[0:1, :]))
                dve.wait_ge(rows_turned, 2)
                V.tensor_copy(src_t[:, NT - 1:NT - 1 + TG * P], psum_t[:, 0, :])
                V.memset(dst_t[:, NT - 1 + TG * P:SPAD], PADF)
                link(V.tensor_copy(dst_t[:, NT - 1:NT - 1 + TG * P], psum_t[:, 1, :]))
                V.tensor_copy(head_src[:, :], psum_t[:, 0, 0:NT])
                V.tensor_copy(head_dst[:, :], psum_t[:, 1, 0:NT])
                V.memset(fsrc, 0.0)
                link(V.tensor_scalar(step_dst[:, :], bstep, -float(P), None, ALU.mult))
                for b in range(NT):
                    lo = NT - 1 - b
                    for table, sink in ((src_t, fsrc), (dst_t, step_dst[:, :])):
                        link(V.scalar_tensor_tensor(out=hit, in0=bstep, scalar=float(b), in1=table[:, lo:lo + TABLE],
                                                    op0=ALU.is_equal, op1=ALU.mult))
                        link(V.tensor_tensor(sink, sink, hit, ALU.add))
                link(V.tensor_copy(step_src[:, :], fsrc))
                dve.wait_ge(runs_loaded, 112)
                link(V.tensor_tensor(run_cut[:, :], cur_i, prev_i, ALU.not_equal))
                link(V.tensor_scalar(run_cut[:, :], run_cut[:, :], -BIG, None, ALU.mult))
                link(V.tensor_scalar(part_i, run_src[:, :], P - 1, None, ALU.bitwise_and))
                link(V.tensor_copy(run_place[:, :], part_i))
                link(V.tensor_copy(run_tile[:, :], run_src[:, :]))
                link(V.tensor_tensor(run_tile[:, :], run_tile[:, :], run_place[:, :], ALU.subtract))
                link(V.tensor_scalar(run_tile[:, :], run_tile[:, :], 1.0 / P, None, ALU.mult))
                V.memset(acc[:, 0:16], 0.0).then_inc(tables_ready, 1)
                dve.wait_ge(tables_ready, 1)

        def onehot_b(slot, k):
            return onehot[:, slot, k, :].bitcast(BF16)[:, 1:2 * P:2]

        def split_thirds(link, V, value, parts):
            for i in range(3):
                link(V.tensor_copy(parts[i], value))
                if i < 2:
                    link(V.tensor_tensor(value, value, parts[i], ALU.subtract))

        def project(name, source, w):
            staged = sem(name + "_staged")
            turned = sem(name + "_turned")
            copied = sem(name + "_copied")
            product = sem(name + "_product")
            stored = sem(name + "_stored")
            gate = sem(name + "_gate")
            stage = acc[:, 0:CH * D]
            xt = acc[:, CH * D:2 * CH * D]
            turn = psum_t[:, :, :].rearrange("p a b -> p (a b)")
            prod = psum_a[:, :, :].rearrange("p a b -> p (a b)")[:, 0:CH * D]
            src_flat = source[:, :, :].rearrange("p b d -> p (b d)")
            turn_e = psum_e[:, 0, 0:D]
            with nc.Block() as block:
                @block.scalar
                def _(act):
                    with act.Fori(0, NT // CH) as c:
                        nc.scalar.copy(stage, src_flat[:, bass.ds(c * (CH * D), CH * D)]).then_inc(staged, 1)
                        act.wait_ge(turned, c + 1)
                        nc.scalar.copy(xt[:, 0:4 * D], turn).then_inc(copied, 1)
                        nc.scalar.copy(xt[:, 4 * D:5 * D], turn_e).then_inc(copied, 1)
                        act.wait_ge(product, c + 1)
                        act.sem_inc(gate, 1)
                        for t in range(CH):
                            nc.scalar.copy(feat[:, bass.ds(c * (CH * SW) + t * SW, D)],
                                           prod[:, t * D:(t + 1) * D]).then_inc(stored, 1)

                @block.tensor
                def _(pe):
                    with pe.Fori(0, NT // CH) as c:
                        pe.wait_ge(staged, c + 1)
                        for t in range(CH):
                            for k in range(2):
                                at = (2 * t + k) * P
                                o = turn[:, at:at + P] if t < 4 else turn_e[:, at - 8 * P:at - 7 * P]
                                last = nc.tensor.transpose(o, stage[:, at:at + P], ident[:, :])
                        last.then_inc(turned, 1)
                        pe.wait_ge(copied, c * 2 + 2)
                        for t in range(CH):
                            for k in range(2):
                                last = nc.tensor.matmul(prod[:, t * D:(t + 1) * D], xt[:, (2 * t + k) * P:(2 * t + k + 1) * P],
                                                        weights[:, w, k, :], start=(k == 0), stop=(k == 1))
                        last.then_inc(product, 1)
                        pe.wait_ge(stored, c * CH + CH)

        def edge_pass(name, table, heads, passes):
            width = D + heads if heads else D
            W = D + heads if heads else D + 1
            fetched = [sem(f"{name}_fetched{a}") for a in range(RING)]
            idx_copied = sem(name + "_e_idx_copied")
            gate = sem(name + "_e_gate")
            oh_ready = sem(name + "_e_oh_ready")
            t_done = sem(name + "_e_t_done")
            oht_ready = sem(name + "_e_oht_ready")
            ex_done = sem(name + "_e_ex_done")
            z_ready = sem(name + "_e_z_ready")
            w_ready = sem(name + "_e_w_ready")
            wm_ready = sem(name + "_e_wm_ready")
            agg_done = sem(name + "_e_agg_done")
            acc_done = sem(name + "_e_acc_done")
            chain = sem(name + "_e_chain")
            term_ready = sem(name + "_e_term_ready")
            table_ready = sem(name + "_e_table_ready")
            acc_clear = sem(name + "_e_acc_clear")
            ones_set = sem(name + "_e_ones_set")
            pass_open = sem(name + "_e_pass_open")
            total_added = sem(name + "_e_total_added")
            NSTEP = GROUPS * HALF
            OHS = GROUPS + AHEAD
            EC = NT // CH

            def tiles_of(engine, regs, g):
                engine.reg_load(regs, step_tile[0:1, bass.ds(g * HALF, HALF)])
                return [engine.snap(r, min_val=0, max_val=NT - 1) for r in regs]

            def loop_passes(eng, body):
                if passes == 1:
                    body(0)
                else:
                    with eng.Fori(0, passes) as r:
                        body(r)

            def loop_groups(eng, group):
                for a in range(RING):
                    group(0, a, True, False)
                with eng.Fori(1, TURNS - 1) as i:
                    for a in range(RING):
                        group(i, a, False, False)
                for a in range(RING):
                    group(TURNS - 1, a, False, True)

            with nc.Block() as block:
                if not heads:
                    @block.sync
                    def _(sp):
                        def one(r):
                            for c in range(EC):
                                sp.wait_ge(term_ready, r * EC + c + 1)
                                sp.dma_start(rows(table)[:, c * CH:(c + 1) * CH, :],
                                             feat3[:, c * CH:(c + 1) * CH, 0:D]).then_inc(table_ready, 16)
                        loop_passes(sp, one)
                        sp.wait_ge(table_ready, 16 * EC * passes)

                @block.gpsimd
                def _(pool):
                    def one(r):
                        with pool.Fori(0, TURNS) as i:
                            for a in range(RING):
                                pool.wait_ge(idx_copied, r * GROUPS + RING * i + a + 1)
                                pool.sem_inc(gate, 1)
                                for k in range(HALF):
                                    s = a * HALF + k
                                    pool.indirect_dma_start(
                                        out=msg[:, s, 0:width], out_offset=None, in_=table[:, :],
                                        in_offset=bass.IndirectOffsetOnAxis(ap=idx_ring[:, s:s + 1], axis=0)
                                    ).then_inc(fetched[a], 16)
                        if not heads:
                            pool.wait_ge(term_ready, r * EC + EC)
                            pool.sem_inc(gate, 1)
                            nc.gpsimd.memset(acc[:, :], 0.0).then_inc(acc_clear, 1)
                            pool.wait_ge(table_ready, (r * EC + EC) * 16)
                            pool.sem_inc(gate, 1)
                    if not heads:
                        nc.gpsimd.memset(msg[:, :, D:D + 1], 1.0).then_inc(ones_set, 1)
                        nc.gpsimd.memset(acc[:, :], 0.0).then_inc(acc_clear, 1)
                    loop_passes(pool, one)

                @block.tensor
                def _(pe):
                    if not heads:
                        pe.wait_ge(ones_set, 1)
                    regs = [pe.alloc_register(f"{name}_pe_tile{k}") for k in range(HALF)]

                    def turn(g, a):
                        pe.wait_ge(oh_ready, g + 1)
                        for k in range(HALF):
                            last = nc.tensor.transpose(psum_tb[:, a % 2, k * P:(k + 1) * P], onehot_b(a % OHR, k), ident_b[:, :])
                        last.then_inc(t_done, 1)

                    def expand(g, a, tiles):
                        pe.wait_ge(oht_ready, g + 1)
                        for k in range(HALF):
                            last = nc.tensor.matmul(psum_e[:, a % 2, k * 16:(k + 1) * 16], onehot_t[:, a % 2, k, :],
                                                    node_ad[:, bass.ds(tiles[k] * 16, 16)], start=True, stop=True)
                        last.then_inc(ex_done, 1)

                    def one(r):
                        def group(i, a, first, last):
                            g = RING * i + a
                            if heads:
                                tiles = tiles_of(pe, regs, g + AHEAD - 1)
                                pe.wait_ge(z_ready, g + AHEAD - 2)
                                expand(g + AHEAD - 1, (a + AHEAD - 1) % RING, tiles)
                            else:
                                pe.wait_ge(oh_ready, r * OHS + g + 1)
                                pe.wait_ge(fetched[a], (r * TURNS + i + 1) * (16 * HALF))
                            for k in range(HALF):
                                if not (first and a == 0):
                                    pe.wait_ge(acc_done, r * NSTEP + (g - 1) * HALF + k + 1)
                                if heads:
                                    pe.wait_ge(wm_ready, g * HALF + k + 1)
                                nc.tensor.matmul(psum_a[:, k, 0:W], onehot[:, a % OHR, k, :], msg[:, a * HALF + k, 0:W],
                                                 start=True, stop=True).then_inc(agg_done, 1)
                            if heads:
                                pe.wait_ge(oht_ready, g + AHEAD - 1)
                                turn(g + AHEAD, (a + AHEAD) % RING)

                        if heads:
                            turn(0, 0)
                            turn(1, 1)
                            expand(0, 0, tiles_of(pe, regs, 0))
                            turn(2, 2)
                            tiles = tiles_of(pe, regs, 1)
                            expand(1, 1, tiles)
                        else:
                            pe.wait_ge(pass_open, r + 1)
                        loop_groups(pe, group)
                    loop_passes(pe, one)

                @block.scalar
                def _(act):
                    def copy_indices(g, a):
                        nc.scalar.copy(idx_ring[:, a * HALF:(a + 1) * HALF],
                                       step_src[:, bass.ds(g * HALF, HALF)]).then_inc(idx_copied, 1)

                    def indices_only(r):
                        act.wait_ge(pass_open, r + 1)
                        act.sem_inc(gate, 1)
                        for a in range(RING):
                            copy_indices(a, a)
                        with act.Fori(1, TURNS) as i:
                            for a in range(RING):
                                g = RING * i + a
                                act.wait_ge(agg_done, r * NSTEP + (g - RING + 1) * HALF)
                                act.sem_inc(gate, 1)
                                copy_indices(g, a)

                    def copy_turned(g, a):
                        act.wait_ge(t_done, g + 1)
                        nc.scalar.copy(onehot_t[:, a % 2, :, :].rearrange("p k e -> p (k e)"),
                                       psum_tb[:, a % 2, 0:HALF * P]).then_inc(oht_ready, 1)

                    def exp(g, a):
                        act.wait_ge(z_ready, g + 1)
                        nc.scalar.activation(msg[:, a * HALF:(a + 1) * HALF, D:D + heads], z[:, a % 2, :, 0:heads],
                                             ACT.Exp).then_inc(w_ready, 1)

                    def group(i, a, first, last):
                        g = RING * i + a
                        if not (last and a == RING - 1):
                            exp(g + 1, (a + 1) % RING)
                        if not (first and a == 0):
                            act.wait_ge(agg_done, g * HALF)
                            act.sem_inc(gate, 1)
                            copy_indices(g - 1 + RING, (a - 1) % RING)
                        act.wait_ge(ex_done, g + AHEAD - 1)
                        copy_turned(g + AHEAD, (a + AHEAD) % RING)

                    if not heads:
                        loop_passes(act, indices_only)
                    else:
                        for a in range(RING):
                            copy_indices(a, a)
                        copy_turned(0, 0)
                        copy_turned(1, 1)
                        act.wait_ge(ex_done, 1)
                        copy_turned(2, 2)
                        exp(0, 0)
                        loop_groups(act, group)

                @block.vector
                def _(dve):
                    V = nc.vector
                    ZCH = 3
                    regs = [dve.alloc_register(f"{name}_dve_tile{k}") for k in range(HALF)]

                    def score_step(n, g, turn, a):
                        ex = psum_e[:, a % 2, 0:HALF * 16].rearrange("p (k w) -> p k w", w=16)
                        zz = z[:, a % 2, :, 0:heads]
                        if n == 0:
                            dve.wait_ge(fetched[a], (turn + 1) * (16 * HALF))
                            dve.wait_ge(ex_done, g + 1)
                            V.tensor_tensor(zz, msg[:, a * HALF:(a + 1) * HALF, D:D + heads],
                                            ex[:, :, 0:heads], ALU.add).then_inc(chain, 1)
                            return
                        dve.wait_ge(chain, g * ZCH + n)
                        if n == 1:
                            V.scalar_tensor_tensor(out=zz, in0=zz, scalar=0.2, in1=zz,
                                                   op0=ALU.mult, op1=ALU.max).then_inc(chain, 1)
                        elif n == 2:
                            V.tensor_tensor(zz, zz, ex[:, :, 8:8 + heads], ALU.subtract).then_inc(chain, 1)
                        else:
                            V.tensor_scalar(zz, zz, 0.0, None, ALU.min).then_inc(z_ready, 1)

                    def weigh(g, a, k):
                        if k == 0:
                            dve.wait_ge(w_ready, g + 1)
                        m = msg[:, a * HALF + k, 0:D].rearrange("p (h c) -> p h c", h=heads)
                        w = msg[:, a * HALF + k, D:D + heads].unsqueeze(2).to_broadcast([P, heads, D // heads])
                        V.tensor_tensor(m, m, w, ALU.mult).then_inc(wm_ready, 1)

                    def make_onehot(g, a):
                        V.tensor_tensor(onehot[:, a % OHR, :, :], iota_n[:, :].unsqueeze(1).to_broadcast([P, HALF, P]),
                                        step_dst[:, bass.ds(g * HALF, HALF)].unsqueeze(2).to_broadcast([P, HALF, P]),
                                        ALU.is_equal).then_inc(oh_ready, 1)

                    def one(r):
                        def add(g, k, tile, nothing_before=False):
                            if not nothing_before:
                                dve.wait_ge(acc_done, r * NSTEP + g * HALF + k)
                            dve.wait_ge(agg_done, r * NSTEP + g * HALF + k + 1)
                            at = acc[:, bass.ds(tile * SW, W)]
                            V.tensor_tensor(at, at, psum_a[:, k, 0:W], ALU.add).then_inc(acc_done, 1)

                        def group(i, a, first, last):
                            g = RING * i + a
                            adds = not (first and a == 0)
                            if adds:
                                tiles = tiles_of(dve, regs, g - 1)
                            for k in range(HALF):
                                if heads:
                                    weigh(g, a, k)
                                if adds:
                                    add(g - 1, k, tiles[k], first and a == 1 and k == 0)
                                if heads and not (last and a == RING - 1):
                                    score_step(k, g + 1, i + 1 if a == RING - 1 else i, (a + 1) % RING)
                            make_onehot(g + AHEAD, (a + AHEAD) % RING)

                        if not heads:
                            V.memset(stat[:, 0, 0:1], 0.0).then_inc(pass_open, 1)
                        for g in range(AHEAD):
                            make_onehot(g, g)
                        if heads:
                            for n in range(4):
                                score_step(n, 0, 0, 0)
                        else:
                            dve.wait_ge(acc_clear, r + 1)
                        loop_groups(dve, group)
                        tiles = tiles_of(dve, regs, GROUPS - 1)
                        for k in range(HALF):
                            add(GROUPS - 1, k, tiles[k])
                        dve.wait_ge(acc_done, r * NSTEP + NSTEP)
                        if heads:
                            return
                        ECH = 4
                        V.tensor_copy(deg[:, :], acc3[:, :, D]).then_inc(chain, 1)
                        dve.wait_ge(chain, r * ECH + 1)
                        V.tensor_scalar(invdeg[:, :], deg[:, :], 1.0, None, ALU.max).then_inc(chain, 1)
                        dve.wait_ge(chain, r * ECH + 2)
                        V.reciprocal(invdeg[:, :], invdeg[:, :]).then_inc(chain, 1)
                        dve.wait_ge(chain, r * ECH + 3)
                        V.tensor_scalar(invdeg[:, :], invdeg[:, :], kinv[:, bass.ds(r, 1)], None, ALU.mult).then_inc(chain, 1)
                        dve.wait_ge(chain, r * ECH + 4)
                        for c in range(EC):
                            b = slice(c * CH, (c + 1) * CH)
                            V.tensor_tensor(feat3[:, b, 0:D], acc3[:, b, 0:D],
                                            invdeg[:, b].unsqueeze(2).to_broadcast([P, CH, D]), ALU.mult).then_inc(term_ready, 1)
                        dve.wait_ge(term_ready, r * EC + EC)
                        V.tensor_tensor(total[:, :, :], total[:, :, :], feat3[:, :, 0:D], ALU.add).then_inc(total_added, 1)
                        dve.wait_ge(table_ready, (r * EC + EC) * 16)
                        dve.wait_ge(total_added, r + 1)
                    loop_passes(dve, one)

        end_phase()
        project("in", x, 0)
        end_phase()
        c0 = sem("c0")
        e0_ready = sem("e0_ready")
        e0_done = sem("e0_done")
        h0_ready = sem("h0_ready")
        h0_stored = sem("h0_stored")
        with nc.Block() as block:
            @block.vector
            def _(dve):
                V = nc.vector
                V.tensor_tensor(feat3[:, :, 0:D], feat3[:, :, 0:D],
                                bias[:, 0, :].unsqueeze(1).to_broadcast([P, NT, D]), ALU.add).then_inc(e0_ready, 1)
                dve.wait_ge(e0_done, 1)
                V.tensor_scalar(tmp, tmp, 1.0, None, ALU.add).then_inc(c0, 1)
                dve.wait_ge(c0, 1)
                V.reciprocal(tmp, tmp).then_inc(c0, 1)
                dve.wait_ge(c0, 2)
                V.tensor_tensor(total[:, :, :], feat3[:, :, 0:D], tmp3, ALU.mult).then_inc(h0_ready, 1)

            @block.scalar
            def _(act):
                act.wait_ge(e0_ready, 1)
                nc.scalar.activation(tmp3, feat3[:, :, 0:D], ACT.Exp, scale=-1.0).then_inc(e0_done, 1)

            @block.sync
            def _(sp):
                sp.wait_ge(h0_ready, 1)
                sp.dma_start(rows(t_term), total[:, :, :]).then_inc(h0_stored, 16)
                sp.wait_ge(h0_stored, 16)
        end_phase()

        edge_pass("diffuse", t_term, 0, KSTEPS)
        end_phase()

        def norm_steps(link, ask_act, y):
            V = nc.vector
            link(V.tensor_reduce(stat[:, 0, :], y, AX.X, ALU.add))
            link(V.tensor_scalar(stat[:, 1, :], stat[:, 0, :], 1.0 / D, None, ALU.mult))
            ask_act(V.tensor_tensor(y, y, stat[:, 1, :].unsqueeze(2).to_broadcast([P, NT, D]), ALU.subtract))
            link(V.tensor_reduce(stat[:, 2, :], tmp3, AX.X, ALU.add))
            ask_act(V.tensor_scalar(stat[:, 3, :], stat[:, 2, :], 1.0 / D, EPS_LN, ALU.mult, ALU.add))
            link(V.reciprocal(stat[:, 0, :], stat[:, 3, :]))
            link(V.tensor_tensor(x[:, :, :], y, stat[:, 0, :].unsqueeze(2).to_broadcast([P, NT, D]), ALU.mult))

        def finish(name, kind, nh=0, bias_row=0):
            chain = sem(name + "_chain")
            asked = sem(name + "_asked")
            answered = sem(name + "_answered")
            stored = sem(name + "_stored")
            with nc.Block() as block:
                @block.vector
                def _(dve):
                    V = nc.vector
                    n = [0, 0]

                    def link(ins):
                        n[0] += 1
                        ins.then_inc(chain, 1)
                        dve.wait_ge(chain, n[0])

                    def ask_act(ins):
                        n[1] += 1
                        ins.then_inc(asked, 1)
                        dve.wait_ge(answered, n[1])

                    y = total[:, :, :]
                    if kind == "linear":
                        link(V.tensor_tensor(y, feat3[:, :, 0:D], bias[:, 1, :].unsqueeze(1).to_broadcast([P, NT, D]), ALU.add))
                    elif kind in ("elu", "relu"):
                        link(V.tensor_scalar(mx[:, :, 0:nh], acc3[:, :, D:D + nh], 1e-16, None, ALU.add))
                        link(V.reciprocal(mx[:, :, 0:nh], mx[:, :, 0:nh]))
                        for h in range(nh):
                            c = D // nh
                            V.tensor_tensor(y[:, :, h * c:(h + 1) * c], acc3[:, :, h * c:(h + 1) * c],
                                            mx[:, :, h:h + 1].to_broadcast([P, NT, c]), ALU.mult).then_inc(chain, 1)
                        n[0] += nh
                        dve.wait_ge(chain, n[0])
                        link(V.tensor_tensor(y, y, bias[:, bias_row, :].unsqueeze(1).to_broadcast([P, NT, D]), ALU.add))
                        if kind == "elu":
                            ask_act(V.tensor_scalar(tmp3, y, 0.0, None, ALU.min))
                            link(V.scalar_tensor_tensor(out=y, in0=y, scalar=0.0, in1=tmp3, op0=ALU.max, op1=ALU.add))
                            link(V.tensor_scalar(y, y, -1.0, None, ALU.add))
                        else:
                            link(V.tensor_scalar(y, y, 0.0, None, ALU.max))
                    else:
                        zz = mx[:, :, 0:nh]
                        c = D // nh
                        link(V.tensor_tensor(zz, zz, acc3[:, :, D:D + nh], ALU.add))
                        link(V.scalar_tensor_tensor(out=zz, in0=zz, scalar=0.01, in1=zz, op0=ALU.mult, op1=ALU.max))
                        link(V.tensor_reduce(stat[:, 0, :], zz, AX.X, ALU.max))
                        ask_act(V.tensor_tensor(zz, zz, stat[:, 0, :].unsqueeze(2).to_broadcast([P, NT, nh]), ALU.subtract))
                        link(V.tensor_reduce(stat[:, 1, :], zz, AX.X, ALU.add))
                        link(V.reciprocal(stat[:, 1, :], stat[:, 1, :]))
                        link(V.tensor_tensor(zz, zz, stat[:, 1, :].unsqueeze(2).to_broadcast([P, NT, nh]), ALU.mult))
                        for h in range(nh):
                            V.tensor_tensor(tmp3[:, :, h * c:(h + 1) * c], acc3[:, :, h * c:(h + 1) * c],
                                            mx[:, :, h:h + 1].to_broadcast([P, NT, c]), ALU.mult).then_inc(chain, 1)
                        n[0] += nh
                        dve.wait_ge(chain, n[0])
                        link(V.tensor_tensor(tmp3[:, :, 0:2 * c], tmp3[:, :, 0:2 * c], tmp3[:, :, 2 * c:4 * c], ALU.add))
                        link(V.tensor_tensor(tmp3[:, :, 0:c], tmp3[:, :, 0:c], tmp3[:, :, c:2 * c], ALU.add))
                        link(V.tensor_tensor(y.rearrange("p b (h c) -> p b h c", h=nh),
                                             x[:, :, :].rearrange("p b (h c) -> p b h c", h=nh),
                                             tmp3[:, :, 0:c].unsqueeze(2).to_broadcast([P, NT, nh, c]), ALU.add))
                    if kind != "edges":
                        link(V.tensor_tensor(y, y, x[:, :, :], ALU.add))
                    norm_steps(link, ask_act, y)
                    V.memset(stat[:, 1, :], 0.0).then_inc(asked, 1)

                @block.scalar
                def _(act):
                    k = 0
                    if kind == "elu":
                        k += 1
                        act.wait_ge(asked, k)
                        nc.scalar.activation(tmp3, tmp3, ACT.Exp).then_inc(answered, 1)
                    if kind == "edges":
                        k += 1
                        act.wait_ge(asked, k)
                        nc.scalar.activation(mx[:, :, 0:nh], mx[:, :, 0:nh], ACT.Exp).then_inc(answered, 1)
                    act.wait_ge(asked, k + 1)
                    nc.scalar.activation(tmp3, total[:, :, :], ACT.Square).then_inc(answered, 1)
                    act.wait_ge(asked, k + 2)
                    nc.scalar.activation(stat[:, 3, :], stat[:, 3, :], ACT.Sqrt).then_inc(answered, 1)
                    if kind == "edges":
                        act.wait_ge(asked, k + 3)
                        act.dma_start(out[0:(NT - 1) * P, :].rearrange("(b p) d -> p b d", p=P), x[:, 0:NT - 1, :]).then_inc(stored, 16)
                        act.dma_start(out[(NT - 1) * P:N, :], x[0:NLAST, NT - 1, :]).then_inc(stored, 16)
                        act.wait_ge(stored, 32)

        def coefficients(name, nh, att_s, att_d, t_feat, t_score, right_in_table=False):
            chain = sem(name + "_cf_chain")
            ready = sem(name + "_cf_ready")
            stored = sem(name + "_cf_stored")
            c = D // nh
            src_score = mx[:, :, 0:nh]
            dst_score = node_ad3[:, :, 0:nh]
            with nc.Block() as block:
                @block.vector
                def _(dve):
                    V = nc.vector
                    n = [0]

                    def link(ins):
                        n[0] += 1
                        ins.then_inc(chain, 1)
                        dve.wait_ge(chain, n[0])
                    for row, sink in ((att_s, src_score), (att_d, dst_score)):
                        link(V.tensor_tensor(tmp3, feat3[:, :, 0:D], att[:, row, :].unsqueeze(1).to_broadcast([P, NT, D]), ALU.mult))
                        link(V.tensor_reduce(sink, tmp3.rearrange("p b (h c) -> p b h c", h=nh), AX.X, ALU.add))
                    V.tensor_copy(feat3[:, :, D:D + nh], dst_score if right_in_table else src_score).then_inc(ready, 1)

                @block.sync
                def _(sp):
                    sp.wait_ge(ready, 1)
                    sp.dma_start(rows(t_feat), feat3[:, :, 0:D + nh]).then_inc(stored, 16)
                    sp.dma_start(rows(t_score), mx[:, :, 0:nh]).then_inc(stored, 16)
                    sp.wait_ge(stored, 32)

        def maxima(name, nh, t_score, t_mx, groups):
            pool_cols = (RUNPAD - groups * HALF) // PTURNS
            assert pool_cols <= MAXPC and groups % OHR == 0
            pool_from = groups * HALF
            fetched = [sem(f"{name}_mf{a}") for a in range(2)]
            idx_copied = sem(name + "_m_idx")
            gate = sem(name + "_m_gate")
            gate_dve = sem(name + "_m_gate_dve")
            moved = sem(name + "_m_moved")
            oh_ready = sem(name + "_m_oh_ready")
            ohq_ready = sem(name + "_m_ohq_ready")
            t_done = sem(name + "_m_t_done")
            oht_ready = sem(name + "_m_oht_ready")
            spread = sem(name + "_m_spread")
            picked = sem(name + "_m_picked")
            picked_half = sem(name + "_m_picked_half")
            selected = sem(name + "_m_selected")
            tab_ready = sem(name + "_m_tab_ready")
            chain = sem(name + "_m_chain")
            scanned = sem(name + "_m_scanned")
            turned = sem(name + "_m_turned")
            carried = sem(name + "_m_carried")
            back = sem(name + "_m_back")
            scores_ready = sem(name + "_m_ready")
            stored = sem(name + "_m_stored")
            got = sem(name + "_m_got")
            asked = sem(name + "_m_asked")
            answered = sem(name + "_m_answered")
            edge_s = tmp[:, 0:RUNPAD * nh]
            scan_s = tmp[:, RUNPAD * MAXH:RUNPAD * MAXH + RUN * nh]
            edge3 = edge_s.rearrange("p (j h) -> p j h", h=nh)
            scan3 = scan_s.rearrange("p (j h) -> p j h", h=nh)
            src_score = feat3[:, :, D:D + nh]
            node_mx = mx[:, :, 0:nh]
            QN = NT * nh
            tab = score_tab[:, 0:QN]
            sel = acc[:, 0:2 * HALF * QN].rearrange("p (s k n) -> p s k n", s=2, k=HALF)
            ohq = acc[:, 2 * HALF * NT * MAXH:2 * HALF * NT * MAXH + 2 * HALF * NT].rearrange(
                "p (s k q) -> p s k q", s=2, k=HALF)

            def loop_groups(eng, group):
                for a in range(OHR):
                    group(a, a, True)
                with eng.Fori(1, groups // OHR) as i:
                    for a in range(OHR):
                        group(i * OHR + a, a, False)

            with nc.Block() as block:
                @block.gpsimd
                def _(pool):
                    with pool.Fori(0, PTURNS) as i:
                        nc.gpsimd.tensor_copy(idx_ring[:, 0:pool_cols],
                                              run_src[:, bass.ds(i * pool_cols + pool_from, pool_cols)]).then_inc(idx_copied, 1)
                        pool.wait_ge(idx_copied, i + 1)
                        pool.sem_inc(gate, 1)
                        for k in range(pool_cols):
                            pool.indirect_dma_start(
                                out=small_ring[:, k * nh:(k + 1) * nh], out_offset=None, in_=t_score[:, :],
                                in_offset=bass.IndirectOffsetOnAxis(ap=idx_ring[:, k:k + 1], axis=0)
                            ).then_inc(fetched[0], 16)
                        pool.wait_ge(fetched[0], (i + 1) * (16 * pool_cols))
                        pool.sem_inc(gate, 1)
                        nc.gpsimd.tensor_copy(edge_s[:, bass.ds((i * pool_cols + pool_from) * nh, pool_cols * nh)],
                                              small_ring[:, 0:pool_cols * nh]).then_inc(moved, 1)
                        pool.wait_ge(moved, i + 1)
                        pool.sem_inc(gate, 1)
                    pool.wait_ge(stored, 16)
                    for b in range(NT):
                        pool.indirect_dma_start(
                            out=mx[:, b, 0:nh], out_offset=None, in_=t_mx[:, :],
                            in_offset=bass.IndirectOffsetOnAxis(ap=last_edge[:, b:b + 1], axis=0)).then_inc(got, 16)

                @block.sync
                def _(sp):
                    sp.wait_ge(scores_ready, 1)
                    sp.dma_start(t_mx.rearrange("(p j) h -> p (j h)", p=P), scan_s).then_inc(stored, 16)
                    sp.wait_ge(stored, 16)

                @block.tensor
                def _(pe):
                    def turn(g, a):
                        pe.wait_ge(oh_ready, g + 1)
                        for k in range(HALF):
                            last = nc.tensor.transpose(psum_tb[:, a % 2, k * P:(k + 1) * P], onehot_b(a, k), ident_b[:, :])
                        last.then_inc(t_done, 1)

                    def spread_scores(g, a):
                        pe.wait_ge(oht_ready, g + 1)
                        for k in range(HALF):
                            for j in range(3):
                                last = nc.tensor.matmul(psum_a[:, 2 * (a % 2) + k // 2, (k % 2) * QN:(k % 2 + 1) * QN],
                                                        onehot_tb[:, a % 2, k * P:(k + 1) * P], score_tab_b[:, j, 0:QN],
                                                        start=(j == 0), stop=(j == 2))
                        last.then_inc(spread, 1)

                    def group(g, a, first):
                        if not (first and a == 0):
                            pe.wait_ge(picked, g)
                        spread_scores(g + 1, (a + 1) % OHR)
                        pe.wait_ge(oht_ready, g + 2)
                        turn(g + AHEAD, (a + AHEAD) % OHR)

                    pe.wait_ge(tab_ready, 1)
                    turn(0, 0)
                    turn(1, 1)
                    spread_scores(0, 0)
                    turn(2, 2)
                    loop_groups(pe, group)
                    pe.wait_ge(scanned, 1)
                    nc.tensor.transpose(psum_e[0:nh, 0, 0:P], carry[:, 0, 0:nh], ident[:, :])
                    nc.tensor.transpose(psum_e[0:nh, 1, 0:P], carry[:, 1, 0:nh], ident[:, :]).then_inc(turned, 1)
                    pe.wait_ge(carried, 1)
                    nc.tensor.transpose(psum_a[:, 0, 0:nh], carry[0:nh, 2, 0:P], ident[0:nh, 0:nh]).then_inc(back, 1)

                @block.scalar
                def _(act):
                    def copy_turned(g, a):
                        act.wait_ge(t_done, g + 1)
                        nc.scalar.copy(onehot_tb[:, a % 2, 0:HALF * P],
                                       psum_tb[:, a % 2, 0:HALF * P]).then_inc(oht_ready, 1)

                    def group(g, a, first):
                        act.wait_ge(spread, g + 2)
                        copy_turned(g + AHEAD, (a + AHEAD) % OHR)

                    copy_turned(0, 0)
                    copy_turned(1, 1)
                    act.wait_ge(spread, 1)
                    copy_turned(2, 2)
                    loop_groups(act, group)
                    act.wait_ge(asked, 1)
                    nc.scalar.activation(wself[:, :, 0:nh], wself[:, :, 0:nh], ACT.Exp).then_inc(answered, 1)

                @block.vector
                def _(dve):
                    V = nc.vector
                    n = [0]

                    def link(ins):
                        n[0] += 1
                        ins.then_inc(chain, 1)
                        dve.wait_ge(chain, n[0])

                    def make_onehot(g, a):
                        V.tensor_tensor(onehot[:, a, :, :], iota_n[:, :].unsqueeze(1).to_broadcast([P, HALF, P]),
                                        run_place[:, bass.ds(g * HALF, HALF)].unsqueeze(2).to_broadcast([P, HALF, P]),
                                        ALU.is_equal).then_inc(oh_ready, 1)

                    def group(g, a, first):
                        b = a % 2
                        if not (first and a < 2):
                            dve.wait_ge(selected, g - 1)
                        V.tensor_tensor(ohq[:, b, :, :], iota_n[:, 0:NT].unsqueeze(1).to_broadcast([P, HALF, NT]),
                                        run_tile[:, bass.ds(g * HALF, HALF)].unsqueeze(2).to_broadcast([P, HALF, NT]),
                                        ALU.is_equal).then_inc(ohq_ready, 1)
                        if not (first and a == 0):
                            dve.wait_ge(t_done, g)
                        make_onehot(g + AHEAD, (a + AHEAD) % OHR)
                        dve.wait_ge(ohq_ready, g + 1)
                        dve.wait_ge(spread, g + 1)
                        for j in range(2):
                            q3 = ohq[:, b, 2 * j:2 * j + 2, :].unsqueeze(3).to_broadcast([P, 2, NT, nh])
                            V.tensor_tensor(sel[:, b, 2 * j:2 * j + 2, :].rearrange("p k (q h) -> p k q h", h=nh),
                                            psum_a[:, 2 * b + j, 0:2 * QN].rearrange("p (k q h) -> p k q h", k=2, h=nh),
                                            q3, ALU.mult).then_inc(picked if j else picked_half, 1)
                        dve.wait_ge(picked_half, g + 1)
                        dve.wait_ge(picked, g + 1)
                        V.tensor_reduce(edge3[:, bass.ds(g * HALF, HALF), :],
                                        sel[:, b, :, :].rearrange("p k (q h) -> p k h q", h=nh), AX.X, ALU.add).then_inc(selected, 1)

                    link(V.tensor_copy(tab.rearrange("p (q h) -> p q h", h=nh), src_score))
                    split_thirds(link, V, tab, [score_tab_b[:, j, 0:QN] for j in range(3)])
                    V.memset(stat[:, 3, :], 0.0).then_inc(tab_ready, 1)
                    make_onehot(0, 0)
                    make_onehot(1, 1)
                    make_onehot(2, 2)
                    loop_groups(dve, group)
                    dve.wait_ge(selected, groups)
                    dve.wait_ge(moved, PTURNS)
                    for h in range(nh):
                        V.tensor_tensor_scan(scan3[:, :, h], run_cut[:, :], edge3[:, 0:RUN, h], -BIG,
                                             ALU.add, ALU.max).then_inc(chain, 1)
                    n[0] += nh
                    dve.wait_ge(chain, n[0])
                    link(V.tensor_reduce(stat[:, 0, 0:1], run_cut[:, :], AX.X, ALU.min))
                    link(V.tensor_copy(carry[:, 0, 0:nh], scan3[:, RUN - 1, :]))
                    V.tensor_copy(carry[:, 1, 0:nh], stat[:, 0, 0:1].to_broadcast([P, nh])).then_inc(scanned, 1)
                    dve.wait_ge(turned, 1)
                    link(V.tensor_copy(carry[0:nh, 3, 0:P], psum_e[0:nh, 1, 0:P]))
                    link(V.memset(carry[0:nh, 2, 0:1], -BIG))
                    V.tensor_tensor_scan(carry[0:nh, 2, 1:P], carry[0:nh, 3, 0:P - 1], psum_e[0:nh, 0, 0:P - 1], -BIG,
                                         ALU.add, ALU.max).then_inc(carried, 1)
                    dve.wait_ge(back, 1)
                    link(V.tensor_copy(stat[:, 1, 0:nh], psum_a[:, 0, 0:nh]))
                    for h in range(nh):
                        V.tensor_tensor_scan(scan3[:, :, h], run_cut[:, :], edge3[:, 0:RUN, h], stat[:, 1, h:h + 1],
                                             ALU.add, ALU.max).then_inc(chain, 1)
                    n[0] += nh
                    dve.wait_ge(chain, n[0])
                    V.memset(stat[:, 2, :], 0.0).then_inc(scores_ready, 1)
                    link(V.tensor_tensor(wself[:, :, 0:nh], src_score, node_ad3[:, :, 0:nh], ALU.add))
                    link(V.scalar_tensor_tensor(out=wself[:, :, 0:nh], in0=wself[:, :, 0:nh], scalar=0.2,
                                                in1=wself[:, :, 0:nh], op0=ALU.mult, op1=ALU.max))
                    dve.wait_ge(got, NT * 16)
                    link(V.tensor_tensor(node_mx, node_mx, no_edge[:, :].unsqueeze(2).to_broadcast([P, NT, nh]), ALU.min))
                    link(V.tensor_tensor(node_mx, node_mx, src_score, ALU.max))
                    link(V.tensor_tensor(node_mx, node_mx, node_ad3[:, :, 0:nh], ALU.add))
                    link(V.scalar_tensor_tensor(out=node_ad3[:, :, 8:8 + nh], in0=node_mx, scalar=0.2, in1=node_mx,
                                                op0=ALU.mult, op1=ALU.max))
                    V.tensor_tensor(wself[:, :, 0:nh], wself[:, :, 0:nh], node_ad3[:, :, 8:8 + nh], ALU.subtract).then_inc(asked, 1)
                    dve.wait_ge(answered, 1)
                    c = D // nh
                    for h in range(nh):
                        V.tensor_tensor(acc3[:, :, h * c:(h + 1) * c], feat3[:, :, h * c:(h + 1) * c],
                                        wself[:, :, h:h + 1].to_broadcast([P, NT, c]), ALU.mult).then_inc(chain, 1)
                    n[0] += nh
                    link(V.tensor_copy(acc3[:, :, D:D + nh], wself[:, :, 0:nh]))

        def last_edges():
            chain = sem("le_chain")
            summed = sem("le_summed")
            with nc.Block() as block:
                @block.tensor
                def _(pe):
                    nc.tensor.matmul(psum_a[:, 0, 0:NT], lower[:, :], deg[:, :], start=True, stop=True).then_inc(summed, 1)
                    nc.tensor.matmul(psum_a[:, 1, 0:NT], ones[:, :], deg[:, :], start=True, stop=True).then_inc(summed, 1)

                @block.vector
                def _(dve):
                    V = nc.vector
                    n = [0]

                    def link(ins):
                        n[0] += 1
                        ins.then_inc(chain, 1)
                        dve.wait_ge(chain, n[0])
                    dve.wait_ge(summed, 2)
                    link(V.memset(stat[:, 1, :], 0.0))
                    link(V.tensor_copy(stat[:, 3, :], psum_a[:, 1, 0:NT]))
                    link(V.tensor_tensor_scan(stat[:, 0, :], stat[:, 3, :], stat[:, 1, :], 0.0, ALU.add, ALU.add))
                    link(V.tensor_tensor(stat[:, 0, :], stat[:, 0, :], stat[:, 3, :], ALU.subtract))
                    link(V.tensor_tensor(stat[:, 0, :], stat[:, 0, :], psum_a[:, 0, 0:NT], ALU.add))
                    link(V.tensor_scalar(stat[:, 0, :], stat[:, 0, :], -1.0, 0.0, ALU.add, ALU.max))
                    link(V.tensor_copy(last_edge[:, :], stat[:, 0, :]))
                    link(V.tensor_scalar(no_edge[:, :], deg[:, :], 0.0, None, ALU.is_gt))
                    link(V.tensor_scalar(no_edge[:, :], no_edge[:, :], 2.0, -1.0, ALU.mult, ALU.add))
                    link(V.tensor_scalar(no_edge[:, :], no_edge[:, :], BIG, None, ALU.mult))

        project("out", total, 1)
        end_phase()
        finish("norm0", "linear")
        end_phase()
        last_edges()
        end_phase()

        project("gat1", x, 2)
        end_phase()
        coefficients("gat1", 8, 0, 1, t_h1, t_as1)
        end_phase()
        maxima("gat1", 8, t_as1, t_mx1, 64)
        end_phase()
        edge_pass("gat1", t_h1, 8, 1)
        end_phase()
        finish("norm1", "elu", 8, 2)
        end_phase()

        project("gat2", x, 3)
        end_phase()
        coefficients("gat2", 4, 2, 3, t_h2, t_as2)
        end_phase()
        maxima("gat2", 4, t_as2, t_mx2, 72)
        end_phase()
        edge_pass("gat2", t_h2, 4, 1)
        end_phase()
        finish("norm2", "relu", 4, 3)
        end_phase()

        project("top", x, 4)
        end_phase()
        coefficients("top", 4, 4, 5, t_h3, t_al3, right_in_table=True)
        end_phase()
        top_got = sem("top_got")
        with nc.Block() as block:
            @block.gpsimd
            def _(pool):
                for b in range(NT):
                    pool.indirect_dma_start(out=acc3[:, b, 0:D + 4], out_offset=None, in_=t_h3[:, :],
                                            in_offset=bass.IndirectOffsetOnAxis(ap=head_dst[:, b:b + 1], axis=0)).then_inc(top_got, 16)
                    pool.indirect_dma_start(out=mx[:, b, 0:4], out_offset=None, in_=t_al3[:, :],
                                            in_offset=bass.IndirectOffsetOnAxis(ap=head_src[:, b:b + 1], axis=0)).then_inc(top_got, 16)
                pool.wait_ge(top_got, 2 * NT * 16)
        end_phase()
        finish("norm3", "edges", 4)
        end_phase()


_INS = ['x', 'src', 'dst', 'L0_gnn_W_in', 'L0_gnn_b_in', 'L0_gnn_W_out', 'L0_gnn_b_out', 'L1_gnn_W0',
        'L1_gnn_att_src0', 'L1_gnn_att_dst0', 'L1_gnn_b0', 'L2_gnn_W', 'L2_gnn_att_src', 'L2_gnn_att_dst',
        'L2_gnn_bias', 'L3_gnn_weight', 'L3_gnn_attn_l', 'L3_gnn_attn_r']


def kernel(**inputs):
    import numpy as _np
    import concourse.bacc as _bacc
    from concourse import mybir as _mybir
    from concourse.bass_utils import run_bass_kernel_spmd as _run

    nc = _bacc.Bacc("TRN2", target_bir_lowering=False, num_devices=1)
    arrays, args = {}, []
    for name in _INS:
        a = _np.ascontiguousarray(inputs[name])
        if "att" in name:
            a = a.reshape(-1)
        arrays[f"in_{name}"] = a
        args.append(nc.dram_tensor(f"in_{name}", a.shape, _mybir.dt.from_np(a.dtype), kind="ExternalInput").ap())
    out = nc.dram_tensor("out", (3125, 256), _mybir.dt.float32, kind="ExternalOutput").ap()
    gnn_kernel(nc, *args, out)
    r = _run(nc, [arrays], core_ids=[0])
    return r.results[0]["out"]
```
